# Optimizing a Trainium2 kernel written in Bass

```python
import numpy as np
import jax
import jax.numpy as jnp

def _softmax(x, axis=-1):
    return jax.nn.softmax(x, axis=axis)

def _gelu(x):
    return jax.nn.gelu(x, approximate=True)

def _silu(x):
    return jax.nn.silu(x)

def _sigmoid(x):
    return jax.nn.sigmoid(x)

def _layernorm(x, axis=-1, eps=1e-05):
    m = jnp.mean(x, axis=axis, keepdims=True)
    v = jnp.var(x, axis=axis, keepdims=True)
    return (x - m) / jnp.sqrt(v + eps)

def _scatter_add(tgt, idx, src, axis=0):
    return tgt.at[idx].add(src)

def _segment_sum(src, seg, n):
    return jax.ops.segment_sum(src, seg, n)
kernel_name = 'mk_gnn_preln_d4_gnn_r32_1009ed'

def setup_inputs(seed: int=0):
    np.random.seed(seed)
    _w = jnp.asarray

    def _rec_inputs():
        import jax
        import jax.numpy as jnp
        _gk = jax.random.key(seed)
        x = -0.0003713 + 1 * jax.random.normal(jax.random.fold_in(_gk, 1), (3125, 128), jnp.float32)
        _s = jax.random.randint(jax.random.fold_in(_gk, 2), (50000,), 0, 3125, jnp.int32)
        _d = jax.random.randint(jax.random.fold_in(_gk, 3), (50000,), 0, 3125, jnp.int32)
        _loop = jnp.arange(3125, dtype=jnp.int32)
        src = jnp.concatenate([_s, _d, _loop])
        dst = jnp.concatenate([_d, _s, _loop])
        _o = jnp.argsort(dst, stable=True)
        src = src[_o]
        dst = dst[_o]
        return (x, src, dst)
    x, src, dst = _rec_inputs()

    def _L0_gnn_setup():
        import jax, jax.numpy as jnp
        import numpy as np
        N_NODES = 3125
        N_EDGES = 20000
        D_IN = 128
        D_HID = 128
        D_OUT = 128
        EPS = 1e-12

        def _sage_conv(x, src, dst, Wl, bl, Wr):
            msgs = x[src]
            agg = jax.ops.segment_sum(msgs, dst, num_segments=N_NODES)
            cnt = jax.ops.segment_sum(jnp.ones((src.shape[0],), x.dtype), dst, num_segments=N_NODES)
            agg = agg / jnp.maximum(cnt, 1.0)[:, None]
            out = agg @ Wl.T + bl + x @ Wr.T
            norm = jnp.sqrt(jnp.sum(out * out, axis=-1, keepdims=True))
            return out / jnp.maximum(norm, EPS)
        key = jax.random.key(seed)
        ks = jax.random.split(key, 8)
        x = jax.random.normal(ks[0], (N_NODES, D_IN), dtype=jnp.float32)
        edge_index = jax.random.randint(ks[1], (2, N_EDGES), 0, N_NODES, dtype=jnp.int64)
        s1 = 1.0 / np.sqrt(D_IN)
        s2 = 1.0 / np.sqrt(D_HID)
        Wl1 = jax.random.uniform(ks[2], (D_HID, D_IN), jnp.float32, -s1, s1)
        bl1 = jax.random.uniform(ks[3], (D_HID,), jnp.float32, -s1, s1)
        Wr1 = jax.random.uniform(ks[4], (D_HID, D_IN), jnp.float32, -s1, s1)
        Wl2 = jax.random.uniform(ks[5], (D_OUT, D_HID), jnp.float32, -s2, s2)
        bl2 = jax.random.uniform(ks[6], (D_OUT,), jnp.float32, -s2, s2)
        Wr2 = jax.random.uniform(ks[7], (D_OUT, D_HID), jnp.float32, -s2, s2)
        return {'x': x, 'edge_index': edge_index, 'Wl1': Wl1, 'bl1': bl1, 'Wr1': Wr1, 'Wl2': Wl2, 'bl2': bl2, 'Wr2': Wr2}
    _L0_gnn_all = _L0_gnn_setup()
    _L0_gnn_in = {k: v for k, v in _L0_gnn_all.items() if k in ('Wl1', 'bl1', 'Wr1', 'Wl2', 'bl2', 'Wr2')}
    del _L0_gnn_all

    def _L1_gnn_setup():
        import jax, jax.numpy as jnp
        import numpy as np
        EPS = 1e-07
        MAX_TANH_ARG = 15.0

        def logmap0(x):
            norm = jnp.linalg.norm(x, axis=-1, keepdims=True)
            norm_c = jnp.clip(norm, EPS, 1.0 - 1e-05)
            return jnp.arctanh(norm_c) * x / jnp.maximum(norm, EPS)

        def expmap0(v):
            norm = jnp.linalg.norm(v, axis=-1, keepdims=True)
            norm_c = jnp.clip(norm, EPS, MAX_TANH_ARG)
            return jnp.tanh(norm_c) * v / jnp.maximum(norm, EPS)
        key = jax.random.key(seed)
        k1, k2, k3, k4, k5, k6 = jax.random.split(key, 6)
        N, E, D_IN, D_OUT = (3125, 50000, 128, 128)
        x = jax.random.normal(k1, (N, D_IN), dtype=jnp.float32)
        edge_index = jax.random.randint(k2, (2, E), 0, N, dtype=jnp.int64)
        s = 1.0 / np.sqrt(D_IN)
        W_self = jax.random.normal(k3, (D_IN, D_OUT), dtype=jnp.float32) * s
        b_self = jax.random.normal(k4, (D_OUT,), dtype=jnp.float32) * s
        W_neigh = jax.random.normal(k5, (D_IN, D_OUT), dtype=jnp.float32) * s
        b_neigh = jax.random.normal(k6, (D_OUT,), dtype=jnp.float32) * s
        return {'x': x, 'edge_index': edge_index, 'W_self': W_self, 'b_self': b_self, 'W_neigh': W_neigh, 'b_neigh': b_neigh}
    _L1_gnn_all = _L1_gnn_setup()
    _L1_gnn_in = {k: v for k, v in _L1_gnn_all.items() if k in ('W_self', 'b_self', 'W_neigh', 'b_neigh')}
    del _L1_gnn_all

    def _L2_gnn_setup():
        import jax, jax.numpy as jnp
        import numpy as np
        N_NODES = 50000
        N_EDGES = 50000
        D_IN = 128
        D_HID = 128
        D_OUT = 128

        def _sage_mean(h, src, dst, inv_deg, W_neigh, W_self, b_self):
            neigh_sum = jax.ops.segment_sum(h[src], dst, num_segments=h.shape[0])
            h_neigh = neigh_sum * inv_deg
            return h @ W_self.T + b_self + h_neigh @ W_neigh.T
        key = jax.random.key(seed)
        ks = jax.random.split(key, 12)
        s = 0.05
        return {'x': jax.random.normal(ks[0], (N_NODES, D_IN), jnp.float32), 'src': jax.random.randint(ks[1], (N_EDGES,), 0, N_NODES), 'dst': jax.random.randint(ks[2], (N_EDGES,), 0, N_NODES), 'W_neigh1': jax.random.normal(ks[3], (D_HID, D_IN), jnp.float32) * s, 'W_self1': jax.random.normal(ks[4], (D_HID, D_IN), jnp.float32) * s, 'b_self1': jnp.zeros((D_HID,), jnp.float32), 'W_neigh2': jax.random.normal(ks[5], (D_HID, D_HID), jnp.float32) * s, 'W_self2': jax.random.normal(ks[6], (D_HID, D_HID), jnp.float32) * s, 'b_self2': jnp.zeros((D_HID,), jnp.float32), 'W_neigh3': jax.random.normal(ks[7], (D_OUT, D_HID), jnp.float32) * s, 'W_self3': jax.random.normal(ks[8], (D_OUT, D_HID), jnp.float32) * s, 'b_self3': jnp.zeros((D_OUT,), jnp.float32)}
    _L2_gnn_all = _L2_gnn_setup()
    _L2_gnn_in = {k: v for k, v in _L2_gnn_all.items() if k in ('W_neigh1', 'W_self1', 'b_self1', 'W_neigh2', 'W_self2', 'b_self2', 'W_neigh3', 'W_self3', 'b_self3')}
    del _L2_gnn_all

    def _L3_gnn_setup():
        import jax, jax.numpy as jnp
        import numpy as np
        N, E, D, H = (50000, 25000, 128, 8)
        DH = D // H
        EPS_LN = 1e-05

        def layer_norm(x, gamma, beta):
            mu = jnp.mean(x, axis=-1, keepdims=True)
            var = jnp.var(x, axis=-1, keepdims=True)
            return (x - mu) * jax.lax.rsqrt(var + EPS_LN) * gamma + beta
        key = jax.random.key(seed)
        ks = jax.random.split(key, 12)
        s = 1.0 / np.sqrt(D)
        x = jax.random.normal(ks[0], (N, D), dtype=jnp.float32)
        src = jax.random.randint(ks[1], (E,), 0, N, dtype=jnp.int32)
        dst = jax.random.randint(ks[2], (E,), 0, N, dtype=jnp.int32)
        Wq = jax.random.normal(ks[3], (D, D), dtype=jnp.float32) * s
        Wk = jax.random.normal(ks[4], (D, D), dtype=jnp.float32) * s
        Wv = jax.random.normal(ks[5], (D, D), dtype=jnp.float32) * s
        Wo = jax.random.normal(ks[6], (D, D), dtype=jnp.float32) * s
        bq = jnp.zeros((D,), jnp.float32)
        bk = jnp.zeros((D,), jnp.float32)
        bv = jnp.zeros((D,), jnp.float32)
        bo = jnp.zeros((D,), jnp.float32)
        gamma1 = jnp.ones((D,), jnp.float32)
        beta1 = jnp.zeros((D,), jnp.float32)
        gamma2 = jnp.ones((D,), jnp.float32)
        beta2 = jnp.zeros((D,), jnp.float32)
        return dict(x=x, src=src, dst=dst, Wq=Wq, bq=bq, Wk=Wk, bk=bk, Wv=Wv, bv=bv, Wo=Wo, bo=bo, gamma1=gamma1, beta1=beta1, gamma2=gamma2, beta2=beta2)
    _L3_gnn_all = _L3_gnn_setup()
    _L3_gnn_in = {k: v for k, v in _L3_gnn_all.items() if k in ('Wq', 'bq', 'Wk', 'bk', 'Wv', 'bv', 'Wo', 'bo', 'gamma1', 'beta1', 'gamma2', 'beta2')}
    del _L3_gnn_all
    return {'x': x, 'src': src, 'dst': dst, 'L0_gnn_Wl1': _L0_gnn_in['Wl1'], 'L0_gnn_bl1': _L0_gnn_in['bl1'], 'L0_gnn_Wr1': _L0_gnn_in['Wr1'], 'L0_gnn_Wl2': _L0_gnn_in['Wl2'], 'L0_gnn_bl2': _L0_gnn_in['bl2'], 'L0_gnn_Wr2': _L0_gnn_in['Wr2'], 'L1_gnn_W_self': _L1_gnn_in['W_self'], 'L1_gnn_b_self': _L1_gnn_in['b_self'], 'L1_gnn_W_neigh': _L1_gnn_in['W_neigh'], 'L1_gnn_b_neigh': _L1_gnn_in['b_neigh'], 'L2_gnn_W_neigh1': _L2_gnn_in['W_neigh1'], 'L2_gnn_W_self1': _L2_gnn_in['W_self1'], 'L2_gnn_b_self1': _L2_gnn_in['b_self1'], 'L2_gnn_W_neigh2': _L2_gnn_in['W_neigh2'], 'L2_gnn_W_self2': _L2_gnn_in['W_self2'], 'L2_gnn_b_self2': _L2_gnn_in['b_self2'], 'L2_gnn_W_neigh3': _L2_gnn_in['W_neigh3'], 'L2_gnn_W_self3': _L2_gnn_in['W_self3'], 'L2_gnn_b_self3': _L2_gnn_in['b_self3'], 'L3_gnn_Wq': _L3_gnn_in['Wq'], 'L3_gnn_bq': _L3_gnn_in['bq'], 'L3_gnn_Wk': _L3_gnn_in['Wk'], 'L3_gnn_bk': _L3_gnn_in['bk'], 'L3_gnn_Wv': _L3_gnn_in['Wv'], 'L3_gnn_bv': _L3_gnn_in['bv'], 'L3_gnn_Wo': _L3_gnn_in['Wo'], 'L3_gnn_bo': _L3_gnn_in['bo'], 'L3_gnn_gamma1': _L3_gnn_in['gamma1'], 'L3_gnn_beta1': _L3_gnn_in['beta1'], 'L3_gnn_gamma2': _L3_gnn_in['gamma2'], 'L3_gnn_beta2': _L3_gnn_in['beta2']}

def reference(x, src, dst, L0_gnn_Wl1, L0_gnn_bl1, L0_gnn_Wr1, L0_gnn_Wl2, L0_gnn_bl2, L0_gnn_Wr2, L1_gnn_W_self, L1_gnn_b_self, L1_gnn_W_neigh, L1_gnn_b_neigh, L2_gnn_W_neigh1, L2_gnn_W_self1, L2_gnn_b_self1, L2_gnn_W_neigh2, L2_gnn_W_self2, L2_gnn_b_self2, L2_gnn_W_neigh3, L2_gnn_W_self3, L2_gnn_b_self3, L3_gnn_Wq, L3_gnn_bq, L3_gnn_Wk, L3_gnn_bk, L3_gnn_Wv, L3_gnn_bv, L3_gnn_Wo, L3_gnn_bo, L3_gnn_gamma1, L3_gnn_beta1, L3_gnn_gamma2, L3_gnn_beta2):
    import jax
    import jax.numpy as jnp

    def _L0_gnn_ref(x, edge_index, Wl1, bl1, Wr1, Wl2, bl2, Wr2):
        import jax, jax.numpy as jnp
        import numpy as np
        N_NODES = 3125
        N_EDGES = 20000
        D_IN = 128
        D_HID = 128
        D_OUT = 128
        EPS = 1e-12

        def _sage_conv(x, src, dst, Wl, bl, Wr):
            msgs = x[src]
            agg = jax.ops.segment_sum(msgs, dst, num_segments=N_NODES)
            cnt = jax.ops.segment_sum(jnp.ones((src.shape[0],), x.dtype), dst, num_segments=N_NODES)
            agg = agg / jnp.maximum(cnt, 1.0)[:, None]
            out = agg @ Wl.T + bl + x @ Wr.T
            norm = jnp.sqrt(jnp.sum(out * out, axis=-1, keepdims=True))
            return out / jnp.maximum(norm, EPS)
        src, dst = (edge_index[0], edge_index[1])
        h = _sage_conv(x, src, dst, Wl1, bl1, Wr1)
        h = jax.nn.relu(h)
        h = _sage_conv(h, src, dst, Wl2, bl2, Wr2)
        return h

    def _L1_gnn_ref(x, edge_index, W_self, b_self, W_neigh, b_neigh):
        import jax, jax.numpy as jnp
        import numpy as np
        EPS = 1e-07
        MAX_TANH_ARG = 15.0

        def logmap0(x):
            norm = jnp.linalg.norm(x, axis=-1, keepdims=True)
            norm_c = jnp.clip(norm, EPS, 1.0 - 1e-05)
            return jnp.arctanh(norm_c) * x / jnp.maximum(norm, EPS)

        def expmap0(v):
            norm = jnp.linalg.norm(v, axis=-1, keepdims=True)
            norm_c = jnp.clip(norm, EPS, MAX_TANH_ARG)
            return jnp.tanh(norm_c) * v / jnp.maximum(norm, EPS)
        num_nodes = x.shape[0]
        src, dst = (edge_index[0], edge_index[1])
        x_tan = logmap0(x)
        h_self = x_tan @ W_self + b_self
        ones = jnp.ones(src.shape[0], dtype=x.dtype)
        degrees = jax.ops.segment_sum(ones, dst, num_segments=num_nodes)
        degrees = jnp.maximum(degrees, 1.0)
        h_neigh = jax.ops.segment_sum(x_tan[src], dst, num_segments=num_nodes)
        h_neigh = h_neigh / degrees[:, None]
        h_neigh = h_neigh @ W_neigh + b_neigh
        return expmap0(h_self + h_neigh)

    def _L2_gnn_ref(x, src, dst, W_neigh1, W_self1, b_self1, W_neigh2, W_self2, b_self2, W_neigh3, W_self3, b_self3):
        import jax, jax.numpy as jnp
        import numpy as np
        N_NODES = 50000
        N_EDGES = 50000
        D_IN = 128
        D_HID = 128
        D_OUT = 128

        def _sage_mean(h, src, dst, inv_deg, W_neigh, W_self, b_self):
            neigh_sum = jax.ops.segment_sum(h[src], dst, num_segments=h.shape[0])
            h_neigh = neigh_sum * inv_deg
            return h @ W_self.T + b_self + h_neigh @ W_neigh.T
        n = x.shape[0]
        deg = jax.ops.segment_sum(jnp.ones((src.shape[0],), x.dtype), dst, num_segments=n)
        inv_deg = (1.0 / jnp.maximum(deg, 1.0))[:, None]
        h = jax.nn.relu(_sage_mean(x, src, dst, inv_deg, W_neigh1, W_self1, b_self1))
        h = jax.nn.relu(_sage_mean(h, src, dst, inv_deg, W_neigh2, W_self2, b_self2))
        h = _sage_mean(h, src, dst, inv_deg, W_neigh3, W_self3, b_self3)
        return h

    def _L3_gnn_ref(x, src, dst, Wq, bq, Wk, bk, Wv, bv, Wo, bo, gamma1, beta1, gamma2, beta2):
        import jax, jax.numpy as jnp
        import numpy as np
        N, E, D, H = (50000, 25000, 128, 8)
        DH = D // H
        EPS_LN = 1e-05

        def layer_norm(x, gamma, beta):
            mu = jnp.mean(x, axis=-1, keepdims=True)
            var = jnp.var(x, axis=-1, keepdims=True)
            return (x - mu) * jax.lax.rsqrt(var + EPS_LN) * gamma + beta
        n = x.shape[0]
        Q = (x @ Wq + bq).reshape(n, H, DH)
        K = (x @ Wk + bk).reshape(n, H, DH)
        V = (x @ Wv + bv).reshape(n, H, DH)
        score = jnp.sum(K[src] * Q[dst], axis=-1) / np.sqrt(DH)
        score = jnp.exp(jnp.clip(score, -5.0, 5.0))
        wV = jax.ops.segment_sum(V[src] * score[..., None], dst, num_segments=n)
        z = jax.ops.segment_sum(score, dst, num_segments=n)
        attn = (wV / (z[..., None] + 0.001)).reshape(n, D)
        h = layer_norm(x + attn, gamma1, beta1)
        h = h + jax.nn.relu(layer_norm(h, gamma2, beta2) @ Wo + bo)
        return h
    edge_index = jnp.stack([src, dst])
    h = jnp.maximum(_layernorm(x, axis=-1), 0.0)
    x = x + _L0_gnn_ref(h, edge_index, L0_gnn_Wl1, L0_gnn_bl1, L0_gnn_Wr1, L0_gnn_Wl2, L0_gnn_bl2, L0_gnn_Wr2)
    h = jnp.maximum(_layernorm(x, axis=-1), 0.0)
    x = x + _L1_gnn_ref(h, edge_index, L1_gnn_W_self, L1_gnn_b_self, L1_gnn_W_neigh, L1_gnn_b_neigh)
    h = jnp.maximum(_layernorm(x, axis=-1), 0.0)
    x = x + _L2_gnn_ref(h, src, dst, L2_gnn_W_neigh1, L2_gnn_W_self1, L2_gnn_b_self1, L2_gnn_W_neigh2, L2_gnn_W_self2, L2_gnn_b_self2, L2_gnn_W_neigh3, L2_gnn_W_self3, L2_gnn_b_self3)
    h = jnp.maximum(_layernorm(x, axis=-1), 0.0)
    x = x + _L3_gnn_ref(h, src, dst, L3_gnn_Wq, L3_gnn_bq, L3_gnn_Wk, L3_gnn_bk, L3_gnn_Wv, L3_gnn_bv, L3_gnn_Wo, L3_gnn_bo, L3_gnn_gamma1, L3_gnn_beta1, L3_gnn_gamma2, L3_gnn_beta2)
    return x

_drawn_inputs = setup_inputs


def setup_inputs(seed=0):
    import zlib

    import numpy as np

    out = dict(_drawn_inputs(seed))
    spreads = {'L2_gnn_b_self1': (0.0, 0.391),
     'L2_gnn_b_self2': (0.0, 0.1),
     'L2_gnn_b_self3': (0.0, 0.1),
     'L3_gnn_bq': (0.0, 0.8),
     'L3_gnn_bk': (0.0, 0.8),
     'L3_gnn_bv': (0.0, 0.1),
     'L3_gnn_bo': (0.0, 0.1),
     'L3_gnn_gamma1': (1.0, 0.2),
     'L3_gnn_beta1': (0.0, 0.1),
     'L3_gnn_gamma2': (1.0, 0.2),
     'L3_gnn_beta2': (0.0, 0.1)}
    factors = {'L0_gnn_bl1': 8.0, 'L1_gnn_b_self': 4.032, 'L1_gnn_b_neigh': 3.817}
    for name, (base, spread) in spreads.items():
        noise = np.random.default_rng([zlib.crc32(name.encode()), seed]).standard_normal(out[name].shape)
        drawn = base * np.exp(spread * noise) if base else spread * noise
        out[name] = jnp.asarray(drawn.astype(out[name].dtype))
    for name, factor in factors.items():
        out[name] = (out[name] * factor).astype(out[name].dtype)
    return out
```

```python
from contextlib import ExitStack

import concourse.bass as bass
from concourse import mybir

F32 = mybir.dt.float32
BF16 = mybir.dt.bfloat16
I32 = mybir.dt.int32
ALU = mybir.AluOpType
ACT = mybir.ActivationFunctionType
AX = mybir.AxisListType
ENG = mybir.EngineType

P = 128
N = 3125
E = 103125
D = 128
H = 8
DH = D // H
NT = -(-N // P)
NP = NT * P
NA = 3136
W = 8
CR = 7
NC = P * CR
UB = 8
TB = -(-(-(-E // P)) // UB)
GC = 4
GU = 6
CU = GC * GU
TA = -(-(-(-E // P)) // CU)
LEAD = 8
TW = D + H
NCE = -(-E // P)
DEG = 255
PAD_DST = 4096
PARTS = 3
YW = PARTS * D
PASSES = 7
X_IN = (0, 2, 3, 6)
X_OUT = (2, 3, 6)
S_IN = (1, 2, 3, 4, 5, 6)
NORMED = (1, 2, 3)
SCALED = (2, 3)
EPS_LN = 1e-05


class Scratch:
    pass


class Num:

    def __init__(self, c, k=None, m=2):
        self.c, self.k, self.m = c, k, m

    def __add__(self, n):
        return Num(self.c + n, self.k, self.m)

    def __sub__(self, n):
        return self + -n

    def value(self, scale=1):
        return self.c * scale if self.k is None else self.k * (self.m * scale) + self.c * scale

    def slot(self, n=2):
        return self.c % n

    def count(self, engine, sem, held=None):
        if self.c > 0:
            engine.wait_ge(sem, self.value())
            if held is not None:
                engine.sem_inc(held, 1)

    def landed(self, engine, sems, held=None):
        if self.c >= 0:
            half = self.c // 2 + 1
            engine.wait_ge(sems[self.slot()], half * 16 if self.k is None else self.k * (self.m * 8) + half * 16)
            if held is not None:
                engine.sem_inc(held, 1)


class Chain:

    def __init__(self, engine, sem):
        self.engine, self.sem, self.steps, self.turned = engine, sem, 0, 0

    def step(self, ins):
        ins.then_inc(self.sem, 1)
        self.steps += 1
        self.engine.wait_ge(self.sem, self.turned + self.steps)

    def loop(self, turns, per_turn, body):
        start = self.steps
        with self.engine.Fori(0, turns) as k:
            self.turned = k * per_turn
            body(k)
            assert self.steps - start == per_turn, (self.steps - start, per_turn)
        self.turned = 0
        self.steps = start + per_turn * turns


def over_tiles(chain, step):
    step(Num(0))
    before = chain.steps
    step(Num(1))
    step(Num(2))

    def body(k):
        step(Num(3, k))
        step(Num(4, k))

    chain.loop((NT - 3) // 2, chain.steps - before, body)


def nth(passes, p, dt):
    return dt + NT * passes.index(p)


def rows(tensor, dt):
    return tensor[bass.ds(dt.value(P), P), :]


ALL = tuple(range(PASSES))


def program(nc, t):
    with ExitStack() as ctx:
        def dram(name, shape, dt=F32):
            return nc.dram_tensor(name, shape, dt, kind="Internal").ap()

        v = Scratch()
        v.base = dram("window_starts", (NC,), I32)
        v.s = [dram(f"self_term{i}", (NP, D)) for i in range(2)]
        v.x = [dram(f"residual{i}", (NP, D)) for i in range(3)]
        v.h = dram("attention_input", (NP, D))
        v.kv = dram("keys_values", (NP, 2 * D))
        v.qt = dram("queries_T", (D, NP))
        v.ident = ctx.enter_context(nc.sbuf_tensor("ident", [P, P], F32))
        v.y_table = dram("y_table", (NP, YW), BF16)
        v.q_table = dram("q_table", (NP, D))
        v.totals = dram("totals", (NP, TW))
        v.odd = ctx.enter_context(nc.sbuf_tensor("odd_edges", [1, 1], I32))
        counts = ctx.enter_context(nc.sbuf_tensor("counts", [P, NT * NA + D], BF16))
        build_counts(nc, t, v, counts)
        odd = nc.values_load(v.odd[0:1, 0:1], min_val=0, max_val=1,
                             skip_runtime_bounds_check_because="a maximum of comparisons")
        with nc.If(odd < 1):
            dense_layers(nc, t, v, counts)
            attention(nc, t, v, counts)
        with nc.Else():
            dense_layers(nc, t, v, counts, by_edge=True)
            attention_by_edge(nc, t, v, counts)


class Room:

    def __init__(self, whole, start=0):
        self.whole, self.at = whole, start

    def take(self, name, shape, dt=F32):
        size = 1
        for n in shape[1:]:
            size *= n
        units = size * (1 if dt == BF16 else 2)
        piece = self.whole[0:shape[0], self.at:self.at + units]
        self.at += units + -units % 16
        assert self.at <= NT * NA + D, name
        piece = piece if dt == BF16 else piece.bitcast(dt)
        names = "abcd"[:len(shape) - 1]
        return piece.rearrange(f"p ({' '.join(names)}) -> p {' '.join(names)}", **dict(zip(names[1:], shape[2:])))


def phase(nc, stack, tag="", clear=False):
    handles = []

    def sb(name, shape, dt=F32):
        return stack.enter_context(nc.sbuf_tensor(name + tag, shape, dt))

    def ps(name, n):
        return [stack.enter_context(nc.psum_tensor(f"{name}{i}{tag}", [P, 512], F32)) for i in range(n)]

    def sem(name):
        if not clear:
            return stack.enter_context(nc.semaphore(name + tag))
        handles.append(nc.alloc_semaphore(name + tag))
        return handles[-1]

    if clear:
        def zero():
            nc.clear_and_free_semaphores(handles)
            nc.all_engine_barrier()

        stack.callback(zero)
    return sb, ps, sem


def build_counts(nc, t, v, counts):
    RH, LH = 4, 4
    KW = NT * W
    with ExitStack() as ctx:
        sb, ps, sem = phase(nc, ctx, "_build", clear=True)
        dst_rows = sb("dst_rows", [P, CR, P], I32)
        dst_cols = sb("dst_cols", [P, NC], I32)
        src_cols = sb("src_cols", [P, NC], I32)
        start_f = sb("start_f", [P, CR])
        start_i = sb("start_i", [P, CR], I32)
        starts = sb("starts", [P, NC], I32)
        src_tile = sb("src_tile", [P, NC], I32)
        src_low = sb("src_low", [P, NC], I32)
        rel = sb("rel", [P, NC])
        key = sb("key", [P, NC])
        neg_low = sb("neg_low", [P, NC])
        iota_i = sb("iota_i", [P, KW], I32)
        iota_b = sb("iota_b", [P, KW], BF16)
        iota_f = sb("iota_f", [P, P])
        one = sb("one", [P, 1])
        right = sb("right", [P, RH, KW], BF16)
        square = sb("square", [P, 2, 2, P])
        left = sb("left", [P, LH, 2, P], BF16)
        share = ps("share", 4)
        flag_bank, = ps("flag_bank", 1)
        flat = sb("flat", [P, 3, NC], I32)
        test = sb("test", [P, 2, NC], BF16)
        worst = sb("worst", [P, 4])
        worst_row = sb("worst_row", [1, P])
        cols = counts[:, 0:NT * NA].rearrange("p (t n) -> p t n", n=NA)

        rows_in, cols_in, starts_out, starts_in = sem("rows_in"), sem("cols_in"), sem("starts_out"), sem("starts_in")
        consts, start_ready, keys_ready = sem("consts"), sem("start_ready"), sem("keys_ready")
        right_ready, left_ready, mm_done, column_sums = sem("right_ready"), sem("left_ready"), sem("mm_done"), sem("column_sums")
        dve_steps, act_steps, pool_steps = sem("dve_steps"), sem("act_steps"), sem("pool_steps")
        flat_in, worst_ready, flag_done = sem("flat_in"), sem("worst_ready"), sem("flag_done")
        held = sem("held")
        block = ctx.enter_context(nc.Block())

        @block.sync
        def _(sp):
            sp.dma_start(dst_rows[:, :, :], t["dst_rows"].rearrange("p (g e) -> p g e", g=CR)).then_inc(rows_in, 16)
            sp.dma_start(dst_cols[:, :], t["dst_cols"]).then_inc(cols_in, 16)
            sp.dma_start(src_cols[:, :], t["src_cols"]).then_inc(cols_in, 16)
            for n, shift in enumerate((0, 1, DEG)):
                sp.dma_start(flat[:, n, :], t["dst_flat"][shift:shift + P * NC].rearrange("(p i) -> p i", p=P)).then_inc(flat_in, 16)
            sp.wait_ge(start_ready, 1)
            sp.dma_start(v.base.rearrange("(p g) -> p g", g=CR), start_i[:, :]).then_inc(starts_out, 16)
            sp.wait_ge(starts_out, 16)
            sp.dma_start(starts[:, :], v.base.partition_broadcast(P)).then_inc(starts_in, 16)

        @block.gpsimd
        def _(pool):
            chain = Chain(pool, pool_steps)
            chain.step(nc.gpsimd.iota(iota_i[:, :], [[1, KW]], base=0, channel_multiplier=0))
            chain.step(nc.gpsimd.tensor_copy(iota_b[:, :], iota_i[:, :]))
            chain.step(nc.gpsimd.tensor_copy(iota_f[:, :], iota_i[:, 0:P]))
            chain.step(nc.gpsimd.memset(one[:, :], 1.0))
            chain.step(nc.gpsimd.memset(v.ident[:, :], 0.0))
            nc.gpsimd.affine_select(out=v.ident[:, :], in_=v.ident[:, :], compare_op=ALU.not_equal, fill=1.0,
                                    base=0, pattern=[[-1, P]], channel_multiplier=1).then_inc(consts, 1)
            half = (NT * NA + D) // 2
            nc.gpsimd.memset(counts[:, 0:half].bitcast(F32), 0.0).then_inc(column_sums, 1)

        @block.vector
        def _(dve):
            chain = Chain(dve, dve_steps)
            half = (NT * NA + D) // 2
            chain.step(nc.vector.memset(counts[:, half:2 * half].bitcast(F32), 0.0))
            dve.wait_ge(rows_in, 16)
            chain.step(nc.vector.tensor_reduce(start_f[:, :], dst_rows[:, :, :], AX.X, ALU.min))
            nc.vector.tensor_scalar(start_i[:, :], start_f[:, :], float(NA - W), None, ALU.min).then_inc(start_ready, 1)
            dve.wait_ge(cols_in, 32)
            chain.step(nc.vector.tensor_scalar(src_tile[:, :], src_cols[:, :], 7, None, ALU.arith_shift_right))
            chain.step(nc.vector.tensor_scalar(src_low[:, :], src_cols[:, :], P - 1, None, ALU.bitwise_and))
            chain.step(nc.vector.tensor_scalar(neg_low[:, :], src_low[:, :], -1.0, None, ALU.mult))
            dve.wait_ge(starts_in, 16)
            chain.step(nc.vector.tensor_tensor(rel[:, :], dst_cols[:, :], starts[:, :], ALU.subtract))
            nc.vector.scalar_tensor_tensor(key[:, :], src_tile[:, :], float(W), rel[:, :], ALU.mult, ALU.add).then_inc(keys_ready, 1)
            dve.wait_ge(keys_ready, 1)
            dve.wait_ge(consts, 1)

            dve.wait_ge(flat_in, 48)
            here, after, far = (flat[:, n, :] for n in range(3))
            fails, more = test[:, 0, :], test[:, 1, :]
            chain.step(nc.vector.tensor_tensor(fails, after, here, ALU.is_lt))
            chain.step(nc.vector.tensor_tensor(more, far, here, ALU.is_equal))
            chain.step(nc.vector.scalar_tensor_tensor(more, here, float(PAD_DST), more, ALU.is_lt, ALU.mult))
            chain.step(nc.vector.tensor_tensor(fails, fails, more, ALU.max))
            chain.step(nc.vector.tensor_scalar(more, rel[:, :], float(W), None, ALU.is_ge))
            chain.step(nc.vector.scalar_tensor_tensor(more, dst_cols[:, :], float(PAD_DST), more, ALU.is_lt, ALU.mult))
            chain.step(nc.vector.tensor_tensor(fails, fails, more, ALU.max))
            chain.step(nc.vector.tensor_reduce(worst[:, 0:1], fails, AX.X, ALU.max))
            chain.step(nc.vector.tensor_copy(worst[:, 1:2], worst[:, 0:1]))
            nc.vector.tensor_copy(worst[:, 2:4], worst[:, 0:2]).then_inc(worst_ready, 1)
            dve.wait_ge(flag_done, 1)
            chain.step(nc.vector.tensor_copy(worst_row[:, :], flag_bank[0:1, 0:P]))
            chain.step(nc.vector.tensor_reduce(worst[0:1, 0:1], worst_row[:, :], AX.X, ALU.max))
            chain.step(nc.vector.tensor_copy(v.odd[:, :], worst[0:1, 0:1]))

            def right_side(c):
                nc.vector.tensor_scalar(right[:, c.slot(RH), :], iota_b[:, :], key[:, bass.ds(c.value(), 1)], None,
                                        ALU.is_equal).then_inc(right_ready, 1)

            right_side(Num(0))
            right_side(Num(1))
            with dve.Fori(0, TB) as k:
                _, first = nc.values_load_multi_w_load_instructions(
                    starts[0:1, bass.ds(k * UB, UB)], engines=(ENG.DVE,), min_val=0, max_val=NA - W,
                    skip_runtime_bounds_check_because="bounded above by the min, below by the node numbers")
                for j in range(UB):
                    c = Num(j, k, UB)
                    right_side(c + 2)
                    (c + 1).count(dve, mm_done)
                    (c + 1).count(dve, column_sums)
                    window = cols[:, :, bass.ds(first[j], W)]
                    nc.vector.tensor_tensor(window, share[j % 4][:, 0:KW].rearrange("p (t w) -> p t w", w=W), window,
                                            ALU.add).then_inc(column_sums, 1)

        @block.scalar
        def _(act):
            chain = Chain(act, act_steps)
            act.wait_ge(consts, 1)
            act.wait_ge(keys_ready, 1)

            def pair(q):
                for n in range(2):
                    c = Num(q.c * 2 + n, q.k, q.m * 2)
                    chain.step(nc.scalar.activation(square[:, q.slot(), n, :], iota_f[:, :], ACT.Square,
                                                    bias=neg_low[:, bass.ds(c.value(), 1)]))
                Num((q.c - LH) * 2 + 2, q.k, q.m * 2).count(act, mm_done)
                nc.scalar.activation(left[:, q.slot(LH), :, :], square[:, q.slot(), :, :], ACT.Relu, bias=one[:, :],
                                     scale=-1.0).then_inc(left_ready, 1)

            for j in range(UB // 2):
                pair(Num(j))

            def turn(k):
                for j in range(UB // 2):
                    pair(Num(UB // 2 + j, k, UB // 2))

            chain.loop(TB - 1, UB, turn)

        @block.tensor
        def _(pe):
            pe.wait_ge(consts, 1)
            pe.wait_ge(worst_ready, 1)
            nc.tensor.matmul(flag_bank[0:4, 0:P], worst[:, :], v.ident[:, :], start=True, stop=True).then_inc(flag_done, 1)
            with pe.Fori(0, TB) as k:
                for j in range(UB):
                    c = Num(j, k, UB)
                    (c + 1).count(pe, right_ready)
                    if j % 2 == 0:
                        Num(j // 2 + 1, k, UB // 2).count(pe, left_ready)
                    nc.tensor.matmul(share[j % 4][:, 0:KW], left[:, (j // 2) % LH, j % 2, :], right[:, j % RH, :],
                                     start=True, stop=True).then_inc(mm_done, 1)


def dense_layers(nc, t, v, counts, by_edge=False):
    with ExitStack() as ctx:
        sb, ps, sem = phase(nc, ctx, "_by_edge" if by_edge else "", clear=by_edge)

        def sems(name):
            return [sem(f"{name}0"), sem(f"{name}1")]

        y3 = [sb(f"y_parts{i}", [P, NT, YW], BF16) for i in range(2)]
        weights = [sb(f"weights{i}", [P, 2 * D]) for i in range(2)]
        qt = y3[0][:, 0:2, 0:2 * D].bitcast(F32)
        wq = y3[0][:, 2, 0:2 * D].bitcast(F32)
        bq = sb("bq", [P, 1])
        bias = [sb("bias_even", [P, 2 * D]), sb("bias_odd", [P, D])]
        inv = sb("inv_count", [P, NT])
        one_col = sb("one_col", [P, 1], BF16)
        one = sb("one_f", [P, 1])
        root = sb("root", [P, 1])
        inv_root = sb("inv_root", [P, 1])
        x_in = sb("x_in", [P, 2, D])
        s_in = sb("s_in", [P, 2, D])
        x_out = sb("x_out", [P, 2, D])
        s_out = sb("s_out", [P, 2, 2 * D])
        z_sum = sb("z_sum", [P, D])
        out = sb("layer_out", [P, 2, D])
        junk = sb("junk", [P, D], BF16)
        plain = sb("plain_h", [P, D])
        h = sb("h", [P, 2, D])
        hT = sb("hT", [P, 2, D])
        ys = sb("ys", [P, 2, 2 * D])
        rest = sb("rest", [P, D])
        stat = sb("stat", [P, 2, 24])
        z_bank, n_bank, t_bank, d_bank = ps("z_bank", 2), ps("n_bank", 2), ps("t_bank", 2), ps("d_bank", 2)

        BN, MV, SS, FAC, CNT, SS2, NRM, CLIP, MAXN, RMAX, LOG1, LOG2, RSTD, NB, VE = (
            slice(0, 6), slice(6, 8), 8, 9, 10, 11, 12, 13, 14, 15, 16, 17, 18, 19, 20)

        w_in, w_q = sems("w_in"), sem("wq_in")
        x_ld, s_ld, x_st, s_st, h_st, q_st = (sems(n) for n in ("x_ld", "s_ld", "x_st", "s_st", "h_st", "q_st"))
        consts = sem("pass_consts")
        z_ready, z_read, out_ready, ss_ready, power_ready = (
            sem(n) for n in ("z_ready", "z_read", "out_ready", "ss_ready", "power_ready"))
        x_ready, var_ready, rstd_ready, nb_ready = (sem(n) for n in ("x_ready", "var_ready", "rstd_ready", "nb_ready"))
        ss2_ready, norm_ready, clip_ready, fn_ready, fac_ready = (
            sem(n) for n in ("ss2_ready", "norm_ready", "clip_ready", "fn_ready", "fac_ready"))
        h_ready, t_done, hT_ready, d_done, ys_ready, y_ready, s_ready = (
            sem(n) for n in ("h_ready", "t_done", "hT_ready", "d_done", "ys_ready", "y_ready", "s_ready"))
        bias_summed = sem("bias_summed")
        z_ld, z_zeroed = (sems("z_ld"), sem("z_zeroed")) if by_edge else (None, None)
        z_in = counts[:, 0:4 * (YW + H)].bitcast(F32).rearrange("p (a n) -> p a n", a=2)
        dve_steps, act_steps, pool_steps, sp_steps = (sem(n) for n in ("p_dve", "p_act", "p_pool", "p_sp"))
        held = sem("held")

        WEIGHTS = [("L0_gnn_Wl1", "L0_gnn_Wr1"), ("L0_gnn_Wl2", "L0_gnn_Wr2"), ("L1_gnn_W_neigh", "L1_gnn_W_self"),
                   ("L2_gnn_W_neigh1", "L2_gnn_W_self1"), ("L2_gnn_W_neigh2", "L2_gnn_W_self2"),
                   ("L2_gnn_W_neigh3", "L2_gnn_W_self3"), ("L3_gnn_Wk", "L3_gnn_Wv")]
        BIASES = [("L0_gnn_bl1",), ("L0_gnn_bl2",), ("L1_gnn_b_self", "L1_gnn_b_neigh"), ("L2_gnn_b_self1",),
                  ("L2_gnn_b_self2",), ("L2_gnn_b_self3",), ("L3_gnn_bk", "L3_gnn_bv")]
        loads = [16 * (2 + len(b)) for b in BIASES]

        def weights_landed(engine, p):
            engine.wait_ge(w_in[p % 2], sum(loads[p % 2:p + 1:2]))

        X_SRC = {0: t["x"], 2: t["x"], 3: v.x[0], 6: v.x[1]}

        sp_chain, pool_chain, pe_chain, act_chain, dve_chain = (
            Chain(e, m) for e, m in ((nc.sync, sp_steps), (nc.gpsimd, pool_steps), (nc.tensor, sp_steps),
                                     (nc.scalar, act_steps), (nc.vector, dve_steps)))

        def sync_passes(sp, passes):
            def load_weights(p):
                for n, name in enumerate(WEIGHTS[p]):
                    sp.dma_start(weights[p % 2][:, n * D:n * D + D], t[name]).then_inc(w_in[p % 2], 16)
                for n, name in enumerate(BIASES[p]):
                    sp.dma_start(bias[p % 2][:, n * D:n * D + D], t[name].partition_broadcast(P)).then_inc(w_in[p % 2], 16)

            def load(p, dt):
                n = nth(ALL, p, dt)
                if p in X_IN:
                    (n - 1).count(sp, h_ready, held)
                    if p > 2:
                        nth(X_OUT, {3: 2, 6: 3}[p], dt).landed(sp, x_st, held)
                    k = nth(X_IN, p, dt)
                    sp.dma_start(x_in[:, k.slot(), :], rows(X_SRC[p], dt)).then_inc(x_ld[k.slot()], 16)
                if p:
                    k = nth(S_IN, p, dt)
                    (k - 1).count(sp, out_ready, held)
                    nth(ALL, p - 1, dt).landed(sp, s_st, held)
                    sp.dma_start(s_in[:, k.slot(), :], rows(v.s[(p - 1) % 2], dt)).then_inc(s_ld[k.slot()], 16)
                if p and by_edge:
                    (k - 1).count(sp, z_ready, held)
                    sp.dma_start(z_in[:, k.slot(), 0:D], rows(v.totals, dt)[:, 0:D]).then_inc(z_ld[k.slot()], 16)
                    sp.dma_start(z_in[:, k.slot(), YW:YW + H], rows(v.totals, dt)[:, D:TW]).then_inc(z_ld[k.slot()], 16)

            def store(p, dt):
                n = nth(ALL, p, dt)
                if p in X_OUT:
                    k = nth(X_OUT, p, dt)
                    (k + 1).count(sp, x_ready, held)
                    sp.dma_start(rows(v.x[X_OUT.index(p)], dt), x_out[:, k.slot(), :]).then_inc(x_st[k.slot()], 16)
                (n + 1).count(sp, s_ready, held)
                if p < 6:
                    sp.dma_start(rows(v.s[p % 2], dt), s_out[:, n.slot(), 0:D]).then_inc(s_st[n.slot()], 16)
                else:
                    sp.dma_start(rows(v.kv, dt), s_out[:, n.slot(), :]).then_inc(s_st[n.slot()], 16)
                    sp.dma_start(rows(v.h, dt), h[:, n.slot(), :]).then_inc(h_st[dt.slot()], 16)
                    (n + 1).count(sp, ys_ready, held)
                    sp.dma_start(v.qt[:, bass.ds(dt.value(P), P)], qt[:, n.slot(), :]).then_inc(q_st[dt.slot()], 16)

            if by_edge:
                sp.wait_ge(z_zeroed, passes[0] + 1)
            if 0 in passes:
                load_weights(0)
                load_weights(1)
                sp.dma_start(bq[:, :], t["L3_gnn_bq"].rearrange("(p a) -> p a", a=1)).then_inc(w_q, 16)
            for p in passes:
                if p == 6:
                    sp.wait_ge(z_ready, NT * 5)
                    sp.dma_start(wq, t["L3_gnn_Wq"]).then_inc(w_q, 16)

                def step(dt):
                    load(p, dt)
                    if dt.c >= 2:
                        store(p, dt - 2)

                over_tiles(sp_chain, step)
                if 1 <= p < 6:
                    sp.wait_ge(d_done, NT * p)
                    sp.wait_ge(s_ready, NT * p)
                    load_weights(p + 1)
                store(p, Num(NT - 2))
                store(p, Num(NT - 1))
            if 6 not in passes:
                return
            for sem_, n in ((s_st, nth(ALL, 6, Num(NT - 1))), (x_st, nth(X_OUT, 6, Num(NT - 1))), (h_st, Num(NT - 1)),
                            (q_st, Num(NT - 1))):
                n.landed(sp, sem_, held)
                (n - 1).landed(sp, sem_, held)

        def pool_passes(pool, passes):
            chain = pool_chain
            if 0 in passes:
                chain.step(nc.gpsimd.memset(one_col[:, :], 1.0))
                chain.step(nc.gpsimd.memset(one[:, :], 1.0))
                chain.step(nc.gpsimd.memset(root[:, :], 0.5))
                nc.gpsimd.memset(inv_root[:, :], -0.5).then_inc(consts, 1)
                pool.wait_ge(consts, 1)
            if by_edge:
                chain.step(nc.gpsimd.memset(z_in[:, :, :], 0.0))
                nc.gpsimd.memset(one[:, :], 1.0).then_inc(z_zeroed, 1)
                pool.wait_ge(z_zeroed, passes[0] + 1)

            def col(n, i):
                return stat[:, n.slot(), i:i + 1]

            def first(p, dt):
                n = nth(ALL, p, dt)
                if p in NORMED:
                    k = nth(NORMED, p, dt)
                    (k + 1).count(pool, ss_ready, held)
                    chain.step(nc.gpsimd.tensor_scalar(col(n, SS), col(n, SS), 1e-14 if p == 3 else 1e-24, None, ALU.max))
                    nc.gpsimd.tensor_tensor(col(n, FAC), col(n, SS), (root if p == 3 else inv_root)[:, :],
                                            ALU.pow).then_inc(power_ready, 1)
                if p in X_IN:
                    k = nth(X_IN, p, dt)
                    (k + 1).count(pool, var_ready, held)
                    chain.step(nc.gpsimd.tensor_scalar(col(n, VE), col(n, MV.start + 1), EPS_LN, None, ALU.add))
                    nc.gpsimd.tensor_tensor(col(n, RSTD), col(n, VE), inv_root[:, :], ALU.pow).then_inc(rstd_ready, 1)
                if p == 2:
                    (dt + 1).count(pool, ss2_ready)
                    nc.gpsimd.tensor_tensor(col(n, NRM), col(n, SS2), root[:, :], ALU.pow).then_inc(norm_ready, 1)

            def second(p, dt):
                n = nth(ALL, p, dt)
                (n + 1).count(pool, ys_ready)
                (n - 2).landed(pool, s_st)
                a, b = (0, 2 * D) if p == 6 else (D, 2 * D)
                nc.gpsimd.tensor_tensor(s_out[:, n.slot(), 0:b - a], ys[:, n.slot(), a:b], bias[p % 2][:, 0:b - a],
                                        ALU.add).then_inc(s_ready, 1)

            for p in passes:
                weights_landed(pool, p)
                if p == 2:
                    nc.gpsimd.tensor_tensor(bias[0][:, 0:D], bias[0][:, 0:D], bias[0][:, D:2 * D], ALU.add).then_inc(bias_summed, 1)
                    pool.wait_ge(bias_summed, 1)

                def step(dt):
                    first(p, dt)
                    if dt.c >= 1:
                        second(p, dt - 1)

                over_tiles(chain, step)
                second(p, Num(NT - 1))

        def tensor_passes(pe, passes):
            chain = pe_chain
            pe.wait_ge(consts, 1)

            def transpose(p, dt):
                n = nth(ALL, p, dt)
                (n + 1).count(pe, h_ready)
                (n - 1).count(pe, hT_ready)
                nc.tensor.transpose(t_bank[n.slot()][:, 0:P], h[:, n.slot(), :], v.ident[:, :]).then_inc(t_done, 1)

            def products(p, dt):
                n = nth(ALL, p, dt)
                (n + 1).count(pe, hT_ready)
                (n - 1).count(pe, ys_ready)
                out_ = d_bank[n.slot()]
                ins = nc.tensor.matmul(out_[:, 0:2 * D], hT[:, n.slot(), :], weights[p % 2][:, :], start=True, stop=True)
                if p == 6:
                    ins = nc.tensor.matmul(out_[:, 2 * D:3 * D], wq, hT[:, n.slot(), :], start=True, stop=True)
                ins.then_inc(d_done, 1)

            def neighbour_sum(p, dt):
                k = nth(S_IN, p, dt)
                (k - 1).count(pe, z_read)
                if by_edge:
                    half = (k.c // 2 + 1) * 32
                    pe.wait_ge(z_ld[k.slot()], half if k.k is None else k.k * 32 + half)
                    ins = nc.tensor.matmul(z_bank[k.slot()][:, 0:YW], v.ident[:, :], z_in[:, k.slot(), 0:YW], start=True, stop=True)
                    if p == 1:
                        ins = nc.tensor.matmul(n_bank[k.slot()][:, 0:1], v.ident[:, :], z_in[:, k.slot(), YW:YW + 1],
                                               start=True, stop=True)
                    ins.then_inc(z_ready, 1)
                    if dt.c >= 1:
                        transpose(p, dt - 1)
                    return
                for s in range(NT):
                    lhs = counts[:, bass.ds(dt.value(P) + s * NA, P)]
                    ins = nc.tensor.matmul(z_bank[k.slot()][:, 0:YW], lhs, y3[(p - 1) % 2][:, s, :],
                                           start=s == 0, stop=s == NT - 1)
                    if p == 1:
                        ins = nc.tensor.matmul(n_bank[k.slot()][:, 0:1], lhs, one_col[:, :],
                                               start=s == 0, stop=s == NT - 1)
                    if s == NT - 1:
                        ins.then_inc(z_ready, 1)
                    if s == 17 and dt.c >= 1:
                        transpose(p, dt - 1)

            for p in passes:
                weights_landed(pe, p)
                if p == 6:
                    pe.wait_ge(w_q, 32)
                pe.wait_ge(y_ready, NT * p) if p else None

                def step(dt):
                    if p:
                        neighbour_sum(p, dt)
                    elif dt.c >= 1:
                        transpose(p, dt - 1)
                    if dt.c >= 1:
                        products(p, dt - 1)

                over_tiles(chain, step)
                transpose(p, Num(NT - 1))
                products(p, Num(NT - 1))

        def scalar_passes(act, passes):
            chain = act_chain
            act.wait_ge(consts, 1)

            def col(n, i):
                return stat[:, n.slot(), i:i + 1]

            def second(p, dt):
                n = nth(ALL, p, dt)
                (n + 1).count(act, t_done)
                (n - 1).count(act, d_done)
                nc.scalar.activation(hT[:, n.slot(), :], t_bank[n.slot()][:, 0:P], ACT.Copy).then_inc(hT_ready, 1)
                (n + 1).count(act, d_done)
                (n - 1).count(act, s_ready)
                if p < 6:
                    (n - 1).count(act, y_ready)
                    chain.step(nc.scalar.activation(ys[:, n.slot(), :], d_bank[n.slot()][:, 0:2 * D], ACT.Copy))
                    nc.scalar.activation(y3[p % 2][:, bass.ds(dt.value(), 1), 0:D].rearrange("p a d -> p (a d)"),
                                         ys[:, n.slot(), 0:D], ACT.Copy).then_inc(ys_ready, 1)
                else:
                    (dt - 2).landed(act, q_st)
                    chain.step(nc.scalar.activation(ys[:, n.slot(), :], d_bank[n.slot()][:, 0:2 * D], ACT.Copy))
                    nc.scalar.activation(qt[:, n.slot(), :], d_bank[n.slot()][:, 2 * D:3 * D], ACT.Identity,
                                         bias=bq[:, :]).then_inc(ys_ready, 1)

            def first(p, dt):
                n = nth(ALL, p, dt)
                if p in NORMED:
                    k = nth(S_IN, p, dt)
                    (k + 1).count(act, out_ready)
                    nc.scalar.activation(junk[:, :], out[:, n.slot(), :], ACT.Square, accum_out=col(n, SS)).then_inc(ss_ready, 1)
                    (nth(NORMED, p, dt) + 1).count(act, ss_ready)
                if p == 3:
                    (nth(SCALED, p, dt) + 1).count(act, clip_ready)
                    nc.scalar.activation(col(n, LOG1), col(n, CLIP), ACT.Tanh).then_inc(fn_ready, 1)
                (n - 1).count(act, t_done)
                if p == 6:
                    (dt - 2).landed(act, h_st)
                h_out = h[:, n.slot(), :]
                if p == 1:
                    (nth(NORMED, p, dt) + 1).count(act, power_ready)
                    nc.scalar.activation(h_out, out[:, n.slot(), :], ACT.Relu, scale=col(n, FAC)).then_inc(h_ready, 1)
                if p in (4, 5):
                    (nth(S_IN, p, dt) + 1).count(act, out_ready)
                    nc.scalar.activation(h_out, out[:, n.slot(), :], ACT.Relu).then_inc(h_ready, 1)
                if p in X_IN:
                    k = nth(X_IN, p, dt)
                    (k + 1).count(act, nb_ready)
                    x_now = x_in[:, k.slot(), :] if p == 0 else x_out[:, nth(X_OUT, p, dt).slot(), :]
                    ins = nc.scalar.activation(plain[:, :] if p == 2 else h_out, x_now, ACT.Relu, bias=col(n, NB),
                                               scale=col(n, RSTD))
                    if p != 2:
                        ins.then_inc(h_ready, 1)
                    else:
                        chain.step(ins)
                        nc.scalar.activation(junk[:, :], plain[:, :], ACT.Square, accum_out=col(n, SS2)).then_inc(ss2_ready, 1)
                        (dt + 1).count(act, ss2_ready)
                        (nth(SCALED, p, dt) + 1).count(act, clip_ready)
                        chain.step(nc.scalar.activation(col(n, LOG1), col(n, CLIP), ACT.Ln, bias=one[:, :]))
                        nc.scalar.activation(col(n, LOG2), col(n, CLIP), ACT.Ln, bias=one[:, :], scale=-1.0).then_inc(fn_ready, 1)
                        (dt + 1).count(act, fac_ready)
                        nc.scalar.activation(h_out, plain[:, :], ACT.Copy, scale=col(n, FAC)).then_inc(h_ready, 1)

            for p in passes:
                if p == 6:
                    act.wait_ge(w_q, 32)

                def step(dt):
                    if dt.c >= 1:
                        second(p, dt - 1)
                    first(p, dt)

                over_tiles(chain, step)
                second(p, Num(NT - 1))

        def vector_passes(dve, passes):
            chain = dve_chain

            def col(n, i):
                return stat[:, n.slot(), i:i + 1]

            def first(p, dt):
                n = nth(ALL, p, dt)
                this = out[:, n.slot(), :]
                if p:
                    k = nth(S_IN, p, dt)
                    z = z_bank[k.slot()]
                    k.count(dve, out_ready)
                    (k + 1).count(dve, z_ready)
                    inv_now = inv[:, bass.ds(dt.value(), 1)]
                    if p == 1:
                        chain.step(nc.vector.tensor_scalar(col(n, CNT), n_bank[k.slot()][:, 0:1], 1.0, None, ALU.max))
                        chain.step(nc.vector.reciprocal(inv_now, col(n, CNT)))
                    nc.vector.tensor_reduce(z_sum[:, :], z[:, 0:YW].rearrange("p (k d) -> p d k", k=PARTS), AX.X,
                                            ALU.add).then_inc(z_read, 1)
                    (k + 1).count(dve, z_read)
                    k.landed(dve, s_ld)
                    nc.vector.scalar_tensor_tensor(this, z_sum[:, :], inv_now, s_in[:, k.slot(), :], ALU.mult,
                                                   ALU.add).then_inc(out_ready, 1)
                if p not in X_IN:
                    return
                k = nth(X_IN, p, dt)
                x_now = x_in[:, k.slot(), :]
                if p:
                    kx = nth(X_OUT, p, dt)
                    x_new = x_out[:, kx.slot(), :]
                    if p in NORMED:
                        (nth(NORMED, p, dt) + 1).count(dve, power_ready)
                    if p == 3:
                        nc.vector.tensor_scalar(col(n, CLIP), col(n, FAC), 15.0, None, ALU.min).then_inc(clip_ready, 1)
                        chain.step(nc.vector.reciprocal(col(n, RMAX), col(n, FAC)))
                        (nth(SCALED, p, dt) + 1).count(dve, fn_ready)
                        chain.step(nc.vector.tensor_tensor(col(n, FAC), col(n, LOG1), col(n, RMAX), ALU.mult))
                    if p == 6:
                        (nth(S_IN, p, dt) + 1).count(dve, out_ready)
                    k.landed(dve, x_ld)
                    (kx - 2).landed(dve, x_st)
                    if p == 6:
                        nc.vector.tensor_tensor(x_new, this, x_now, ALU.add).then_inc(x_ready, 1)
                    else:
                        nc.vector.scalar_tensor_tensor(x_new, this, col(n, FAC), x_now, ALU.mult, ALU.add).then_inc(x_ready, 1)
                    (kx + 1).count(dve, x_ready)
                    x_now = x_new
                else:
                    k.landed(dve, x_ld)
                chain.step(nc.vector.bn_stats(stat[:, n.slot(), BN], x_now))
                dve.sem_inc(held, 1)
                nc.vector.bn_aggr(stat[:, n.slot(), MV], stat[:, n.slot(), BN]).then_inc(var_ready, 1)
                (k + 1).count(dve, rstd_ready)
                nc.vector.tensor_scalar(col(n, NB), col(n, MV.start), col(n, RSTD), -1.0, ALU.mult, ALU.mult).then_inc(nb_ready, 1)
                if p == 2:
                    (dt + 1).count(dve, norm_ready)
                    nc.vector.tensor_scalar(col(n, CLIP), col(n, NRM), 1e-7, 1.0 - 1e-5, ALU.max, ALU.min).then_inc(clip_ready, 1)
                    chain.step(nc.vector.tensor_scalar(col(n, MAXN), col(n, NRM), 1e-7, None, ALU.max))
                    chain.step(nc.vector.reciprocal(col(n, RMAX), col(n, MAXN)))
                    (nth(SCALED, p, dt) + 1).count(dve, fn_ready)
                    chain.step(nc.vector.tensor_tensor(col(n, LOG1), col(n, LOG1), col(n, LOG2), ALU.subtract))
                    nc.vector.tensor_scalar(col(n, FAC), col(n, LOG1), 0.5, col(n, RMAX), ALU.mult, ALU.mult).then_inc(fac_ready, 1)

            def second(p, dt):
                n = nth(ALL, p, dt)
                nth(ALL, p, dt).count(dve, y_ready)
                (n + 1).count(dve, ys_ready)
                part = [y3[p % 2][:, bass.ds(dt.value(), 1), i * D:i * D + D].rearrange("p a d -> p (a d)") for i in range(PARTS)]
                chain.step(nc.vector.tensor_tensor(rest[:, :], ys[:, n.slot(), 0:D], part[0], ALU.subtract))
                chain.step(nc.vector.tensor_copy(part[1], rest[:, :]))
                nc.vector.tensor_tensor(part[2], rest[:, :], part[1], ALU.subtract).then_inc(y_ready, 1)

            for p in passes:
                def step(dt):
                    first(p, dt)
                    if dt.c >= 1 and p < 6:
                        second(p, dt - 1)

                over_tiles(chain, step)
                if p < 6:
                    second(p, Num(NT - 1))

        def run(passes):
            with nc.Block() as block:
                block.sync(lambda sp: sync_passes(sp, passes))
                block.gpsimd(lambda pool: pool_passes(pool, passes))
                block.tensor(lambda pe: tensor_passes(pe, passes))
                block.scalar(lambda act: scalar_passes(act, passes))
                block.vector(lambda dve: vector_passes(dve, passes))

        if not by_edge:
            run(ALL)
            return
        for p in ALL:
            if p:
                sum_by_edge(nc, t, v, counts, z_bank[0], y3[(p - 1) % 2], f"_{p}")
            run((p,))


def attention(nc, t, v, counts):
    GW = GC * W * H
    LAST = GU * TA
    with ExitStack() as ctx:
        room = Room(counts)
        sums = room.take("sums", [P, 2, NP])
        with ExitStack() as edge:
            sb, ps, sem = phase(nc, edge)
            queries = room.take("queries", [P, NP, H])
            qt = sb("qt_all", [P, NP])
            head = sb("head", [P, H])
            src_cols = sb("a_src", [P, NC], I32)
            dst_cols = sb("a_dst", [P, NC], I32)
            starts = sb("a_starts", [P, LEAD + NC], I32)
            rel = sb("a_rel", [P, NC])
            iota_i = sb("a_iota_i", [P, W], I32)
            iota_f = sb("a_iota", [P, W])
            ones = sb("a_ones", [P, P])
            index = sb("index", [P, GU, GC], I32)
            rows_kv = room.take("rows_kv", [P, GU, GC, 2 * D])
            kT = sb("kT", [P, 2, GC * P])
            clipped = sb("clipped", [P, 2, GW])
            weight = sb("weight", [P, 2, GW])
            masked = sb("masked", [P, 2, GW])
            here = sb("here", [P, 2, GC, W])
            picked = sb("picked", [P, 2 * GC * W, H])
            added = sb("added", [P, 2 * GC * W])
            t_bank, s_bank, o_bank = ps("at_bank", 2), ps("as_bank", 2), ps("ao_bank", 2)

            ld = [sem(f"a_ld{i}") for i in range(4)]
            gathered = [sem(f"gathered{i}") for i in range(GU)]
            consts, queries_ready, rel_ready = sem("a_consts"), sem("queries_ready"), sem("rel_ready")
            t_done, kT_ready, s_done, clip_done, exp_done = (sem(n) for n in ("at_done", "kT_ready", "as_done", "clip_done", "exp_done"))
            masked_ready, o_done, picked_ready, index_ready = (sem(n) for n in ("masked_ready", "o_done", "picked_ready", "index_ready"))
            dve_steps, pool_steps = sem("a_dve"), sem("a_pool")
            held = sem("a_held")
            block = edge.enter_context(nc.Block())

            def groups(engine, per_group, chain=None):
                for j in range(GU):
                    per_group(Num(j, None, GU), j)

                def body(k):
                    for j in range(GU):
                        per_group(Num(GU + j, k, GU), j)

                return body

            def first_nodes(engine_type, first_group, k):
                at = k * CU + (LEAD + first_group * GC) if k is not None else LEAD + first_group * GC
                _, regs = nc.values_load_multi_w_load_instructions(
                    starts[0:1, bass.ds(at, CU)], engines=(engine_type,), min_val=0, max_val=NA - W,
                    skip_runtime_bounds_check_because="bounded by the build")
                return regs

            @block.sync
            def _(sp):
                sp.dma_start(src_cols[:, :], t["src_cols"]).then_inc(ld[0], 16)
                sp.dma_start(dst_cols[:, :], t["dst_cols"]).then_inc(ld[1], 16)
                sp.dma_start(starts[:, LEAD:], v.base.partition_broadcast(P)).then_inc(ld[2], 16)
                sp.dma_start(qt[:, :], v.qt).then_inc(ld[3], 16)

            @block.gpsimd
            def _(pool):
                chain = Chain(pool, pool_steps)
                chain.step(nc.gpsimd.memset(head[:, :], 1.0))
                chain.step(nc.gpsimd.affine_select(out=head[:, :], in_=head[:, :], compare_op=ALU.is_ge, fill=0.0,
                                                   base=0, pattern=[[-DH, H]], channel_multiplier=1))
                chain.step(nc.gpsimd.affine_select(out=head[:, :], in_=head[:, :], compare_op=ALU.is_ge, fill=0.0,
                                                   base=DH - 1, pattern=[[DH, H]], channel_multiplier=-1))
                chain.step(nc.gpsimd.iota(iota_i[:, :], [[1, W]], base=0, channel_multiplier=0))
                chain.step(nc.gpsimd.tensor_copy(iota_f[:, :], iota_i[:, :]))
                chain.step(nc.gpsimd.memset(ones[:, :], 1.0))
                chain.step(nc.gpsimd.memset(starts[:, 0:LEAD], 0))
                nc.gpsimd.memset(sums[:, :, :], 0.0).then_inc(consts, 1)

                def gather(g, j):
                    (g + 1).count(pool, index_ready, held)
                    (g - (GU - 1)).count(pool, o_done, held)
                    for c in range(GC):
                        nc.gpsimd.indirect_dma_start(rows_kv[:, j, c, :], None, v.kv,
                                                     bass.IndirectOffsetOnAxis(index[:, j, c:c + 1], 0)).then_inc(gathered[j], 16)

                body = groups(pool, gather)
                with pool.Fori(0, TA - 1) as k:
                    body(k)

            @block.scalar
            def _(act):
                act.wait_ge(ld[0], 16)

                def stage_index(g, j):
                    nc.scalar.activation(index[:, j, :], src_cols[:, bass.ds(g.value(GC), GC)], ACT.Copy).then_inc(index_ready, 1)

                for j in range(GU - 1):
                    stage_index(Num(j), j)

                def step(g, j, load=True, copy=True):
                    if copy:
                        (g + 1).count(act, t_done)
                        (g - 1).count(act, s_done)
                        nc.scalar.activation(kT[:, g.slot(), :], t_bank[g.slot()][:, :], ACT.Copy).then_inc(kT_ready, 1)
                    if load:
                        stage_index(g + (GU - 1), (j - 1) % GU)
                    if g.c >= 1:
                        g.count(act, clip_done)
                        (g - 2).count(act, masked_ready)
                        nc.scalar.activation(weight[:, (g - 1).slot(), :], clipped[:, (g - 1).slot(), :], ACT.Exp).then_inc(exp_done, 1)

                body = groups(act, step)
                if TA > 2:
                    with act.Fori(0, TA - 2) as k:
                        body(k)
                for j in range(GU):
                    step(Num(LAST - GU + j), j, load=j == 0)
                step(Num(LAST), 0, load=False, copy=False)

            @block.tensor
            def _(pe):
                pe.wait_ge(consts, 1)
                pe.wait_ge(queries_ready, 1)
                pe.wait_ge(ld[2], 16)

                def step(g, j, regs, copy=True):
                    if copy:
                        turn = g.c // GU + 1
                        pe.wait_ge(gathered[j], turn * 16 * GC if g.k is None else g.k * (16 * GC) + turn * 16 * GC)
                        (g - 1).count(pe, kT_ready)
                        for c in range(GC):
                            ins = nc.tensor.transpose(t_bank[g.slot()][:, c * P:c * P + P], rows_kv[:, j, c, 0:D], v.ident[:, :])
                        ins.then_inc(t_done, 1)
                    if g.c >= 1 and g.c - 1 < LAST:
                        g1 = g - 1
                        g.count(pe, kT_ready)
                        (g1 - 1).count(pe, clip_done)
                        for c in range(GC):
                            ins = nc.tensor.matmul(s_bank[g1.slot()][:, c * W * H:(c + 1) * W * H],
                                                   kT[:, g1.slot(), c * P:c * P + P],
                                                   queries[:, bass.ds(regs[j * GC + c], W), :].rearrange("p w h -> p (w h)"),
                                                   start=True, stop=True)
                        ins.then_inc(s_done, 1)
                    if g.c >= 2:
                        g2 = g - 2
                        (g2 + 1).count(pe, masked_ready)
                        (g2 - 1).count(pe, picked_ready)
                        for c in range(GC):
                            nc.tensor.matmul(o_bank[g2.slot()][:, c * W * H:(c + 1) * W * H], rows_kv[:, (j - 2) % GU, c, D:2 * D],
                                             masked[:, g2.slot(), c * W * H:(c + 1) * W * H], start=True, stop=True)
                        nc.tensor.matmul(o_bank[g2.slot()][:, GW:2 * GW], ones[:, :], masked[:, g2.slot(), :],
                                         start=True, stop=True).then_inc(o_done, 1)

                regs = first_nodes(ENG.PE, -1, None)
                for j in range(GU):
                    step(Num(j), j, regs)
                with pe.Fori(0, TA - 1) as k:
                    regs = first_nodes(ENG.PE, GU - 1, k)
                    for j in range(GU):
                        step(Num(GU + j, k, GU), j, regs)
                regs = first_nodes(ENG.PE, LAST - 1, None)
                for j in range(2):
                    step(Num(LAST + j), j, regs, copy=False)

            @block.vector
            def _(dve):
                chain = Chain(dve, dve_steps)
                dve.wait_ge(consts, 1)
                dve.wait_ge(ld[1], 16)
                dve.wait_ge(ld[2], 16)
                nc.vector.tensor_tensor(rel[:, :], dst_cols[:, :], starts[:, LEAD:], ALU.subtract).then_inc(rel_ready, 1)
                dve.wait_ge(rel_ready, 1)
                dve.wait_ge(ld[3], 16)
                chain.step(nc.vector.tensor_scalar(qt[:, :], qt[:, :], float(DH) ** -0.5, None, ALU.mult))
                nc.vector.tensor_tensor(queries[:, :, :], qt[:, :].unsqueeze(2).to_broadcast([P, NP, H]),
                                        head[:, :].unsqueeze(1).to_broadcast([P, NP, H]), ALU.mult).then_inc(queries_ready, 1)

                def step(g, j, regs):
                    g1, g2 = g - 1, g - 2
                    if 1 <= g.c <= LAST:
                        chain.step(nc.vector.tensor_tensor(
                            here[:, g1.slot(), :, :], rel[:, bass.ds(g1.value(GC), GC)].unsqueeze(2).to_broadcast([P, GC, W]),
                            iota_f[:, :].unsqueeze(1).to_broadcast([P, GC, W]), ALU.is_equal))
                        g.count(dve, s_done)
                        nc.vector.tensor_scalar(clipped[:, g1.slot(), :], s_bank[g1.slot()][:, 0:GW], -5.0, 5.0, ALU.max,
                                                ALU.min).then_inc(clip_done, 1)
                    if g.c >= 2:
                        (g2 + 1).count(dve, o_done)
                        nc.vector.tensor_tensor(picked[:, :, :], o_bank[g2.slot()][:, :].rearrange("p (n h) -> p n h", h=H),
                                                head[:, :].unsqueeze(1).to_broadcast([P, 2 * GC * W, H]),
                                                ALU.mult).then_inc(picked_ready, 1)
                        (g2 + 1).count(dve, picked_ready)
                        chain.step(nc.vector.tensor_reduce(added[:, :], picked[:, :, :], AX.X, ALU.add))
                        parts = added[:, :].rearrange("p (a c w) -> p a c w", a=2, c=GC)
                        for c in range(GC):
                            window = sums[:, :, bass.ds(regs[j * GC + c], W)]
                            chain.step(nc.vector.tensor_tensor(window, window, parts[:, :, c, :], ALU.add))
                    if 1 <= g.c <= LAST:
                        g.count(dve, exp_done)
                        (g1 - 1).count(dve, o_done)
                        nc.vector.tensor_tensor(masked[:, g1.slot(), :].rearrange("p (n h) -> p n h", h=H),
                                                weight[:, g1.slot(), :].rearrange("p (n h) -> p n h", h=H),
                                                here[:, g1.slot(), :, :].rearrange("p c w -> p (c w)").unsqueeze(2).to_broadcast([P, GC * W, H]),
                                                ALU.mult).then_inc(masked_ready, 1)

                regs = first_nodes(ENG.DVE, -2, None)
                for j in range(GU):
                    step(Num(j), j, regs)

                def turn(k):
                    regs = first_nodes(ENG.DVE, GU - 2, k)
                    for j in range(GU):
                        step(Num(GU + j, k, GU), j, regs)

                chain.loop(TA - 1, GU * (2 + GC), turn)
                regs = first_nodes(ENG.DVE, LAST - 2, None)
                for j in range(2):
                    step(Num(LAST + j), j, regs)

        finish(nc, t, v, sums)


def add_by_edge(nc, t, v, sb, stack, tag, bank, table=None):
    attend = table is None

    _, _, sem = phase(nc, stack, f"_ge{tag}", clear=True)

    width = 2 * D if attend else YW
    dt = F32 if attend else BF16
    src_cols, dst_cols, low_cols = sb("src", [P, NC], I32), sb("dst", [P, NC], I32), sb("low", [P, NC], I32)
    dst_f = sb("dst_f", [P, NC])
    lower = sb("lower", [P, P])
    ones = sb("ones", [P, P])
    zeros = sb("zeros", [P, NT, TW])
    index = sb("index", [P, 2], I32)
    rows_in = sb("rows", [P, width], dt)
    old, new = sb("old", [P, TW]), sb("new", [P, TW])
    dst_row = sb("dst_row", [P, P], I32)
    same, before = sb("same", [P, P], dt), sb("before", [P, P])
    dup, count = sb("dup", [P, 1]), sb("count", [P, 1])
    target = sb("target", [P, 1], I32)
    part_sum = sb("part_sum", [P, D])
    q_rows, prod, score = sb("q_rows", [P, D]), sb("prod", [P, D]), sb("score", [P, H])
    msg = sb("msg", [P, TW])
    cols_in, consts, low_ready, zeroed, tables_ready, landed, row_in, staged = (sem(n) for n in ("cols_in", "consts", "low_ready", "zeroed", "tables_ready", "landed", "row_in", "staged"))
    got, clip_ready, exp_ready, msg_ready = (sem(n) for n in ("got", "clip", "exp", "msg"))
    summed, new_ready, dve_steps, pool_steps, held = (sem(n) for n in ("summed", "new", "dve", "pool", "held"))
    GATHERS = 3 if attend else 2

    def over_chunks(engine, body):
        body(0)
        with engine.Fori(0, NCE - 1) as k:
            body(k + 1)

    def chunk_before(engine, k):
        if not isinstance(k, int):
            engine.wait_ge(landed, k * 16)

    with nc.Block() as block:
        @block.sync
        def _(sp):
            sp.dma_start(src_cols[:, :], t["src_cols"]).then_inc(cols_in, 16)
            sp.dma_start(dst_cols[:, :], t["dst_cols"]).then_inc(cols_in, 16)
            sp.wait_ge(consts, 1)
            sp.dma_start(v.totals.rearrange("(t p) c -> p t c", p=P), zeros[:, :, :]).then_inc(zeroed, 16)
            if table is not None:
                sp.dma_start(v.y_table.rearrange("(t p) c -> p t c", p=P), table[:, :, :]).then_inc(zeroed, 16)
            sp.wait_ge(zeroed, 16 if attend else 32)
            sp.sem_inc(tables_ready, 1)

            def chunk(k):
                chunk_before(sp, k)
                sp.sem_inc(held, 1)
                sp.dma_start(dst_row[:, :], t["dst_flat"][bass.ds(k * P, P)].partition_broadcast(P)).then_inc(row_in, 16)

            over_chunks(sp, chunk)
            sp.wait_ge(landed, NCE * 16)

        @block.gpsimd
        def _(pool):
            chain = Chain(pool, pool_steps)
            chain.step(nc.gpsimd.memset(zeros[:, :, :], 0.0))
            chain.step(nc.gpsimd.memset(ones[:, :], 1.0))
            chain.step(nc.gpsimd.memset(old[:, :], 0.0))
            nc.gpsimd.affine_select(out=lower[:, :], in_=ones[:, :], compare_op=ALU.is_gt, fill=0.0, base=0,
                                    pattern=[[-1, P]], channel_multiplier=1).then_inc(consts, 1)
            pool.wait_ge(tables_ready, 1)

            def chunk(k):
                pool.wait_ge(staged, k + 1)
                pool.sem_inc(held, 1)
                nc.gpsimd.indirect_dma_start(rows_in[:, :], None, v.kv if attend else v.y_table,
                                             bass.IndirectOffsetOnAxis(index[:, 0:1], 0)).then_inc(got, 16)
                nc.gpsimd.indirect_dma_start(old[:, :], None, v.totals, bass.IndirectOffsetOnAxis(index[:, 1:2], 0)).then_inc(got, 16)
                if attend:
                    nc.gpsimd.indirect_dma_start(q_rows[:, :], None, v.q_table,
                                                 bass.IndirectOffsetOnAxis(index[:, 1:2], 0)).then_inc(got, 16)
                pool.wait_ge(new_ready, k + 1)
                pool.sem_inc(held, 1)
                nc.gpsimd.indirect_dma_start(v.totals, bass.IndirectOffsetOnAxis(target[:, :], 0), new[:, :], None,
                                             bounds_check=NP - 1, oob_is_err=False).then_inc(landed, 16)

            over_chunks(pool, chunk)

        @block.scalar
        def _(act):
            act.wait_ge(cols_in, 32)
            act.wait_ge(low_ready, 1)

            def chunk(k):
                chunk_before(act, k)
                nc.scalar.activation(index[:, 0:1], src_cols[:, bass.ds(k, 1)], ACT.Copy).then_inc(held, 1)
                nc.scalar.activation(index[:, 1:2], low_cols[:, bass.ds(k, 1)], ACT.Copy).then_inc(staged, 1)
                if attend:
                    act.wait_ge(clip_ready, k + 1)
                    nc.scalar.activation(msg[:, D:TW], score[:, :], ACT.Exp).then_inc(exp_ready, 1)

            over_chunks(act, chunk)

        @block.tensor
        def _(pe):
            def chunk(k):
                pe.wait_ge(msg_ready, k + 1)
                pe.wait_ge(got, k * (16 * GATHERS) + 16 * GATHERS)
                if attend:
                    nc.tensor.matmul(bank[:, 0:TW], same[:, :], msg[:, :], start=True, stop=True).then_inc(summed, 1)
                else:
                    nc.tensor.matmul(bank[:, 0:YW], same[:, :], rows_in[:, :], start=True, stop=True).then_inc(summed, 1)

            over_chunks(pe, chunk)

        @block.vector
        def _(dve):
            chain = Chain(dve, dve_steps)
            dve.wait_ge(cols_in, 32)
            chain.step(nc.vector.tensor_scalar(low_cols[:, :], dst_cols[:, :], float(NP - 1), None, ALU.min))
            nc.vector.tensor_copy(dst_f[:, :], dst_cols[:, :]).then_inc(low_ready, 1)
            dve.wait_ge(low_ready, 1)
            dve.wait_ge(consts, 1)

            def chunk(k):
                at = bass.ds(k, 1)
                dve.wait_ge(row_in, k * 16 + 16)
                chunk_before(dve, k)
                chain.step(nc.vector.tensor_scalar(same[:, :], dst_row[:, :], dst_f[:, at], None, ALU.is_equal))
                chain.step(nc.vector.tensor_tensor(before[:, :], same[:, :], lower[:, :], ALU.mult))
                chain.step(nc.vector.tensor_reduce(dup[:, :], before[:, :], AX.X, ALU.max))
                chain.step(nc.vector.scalar_tensor_tensor(target[:, :], dup[:, :], float(2 * PAD_DST), dst_f[:, at], ALU.mult, ALU.add))
                if attend:
                    dve.wait_ge(got, k * (16 * GATHERS) + 16 * GATHERS)
                    chain.step(nc.vector.tensor_tensor(prod[:, :], rows_in[:, 0:D], q_rows[:, :], ALU.mult))
                    chain.step(nc.vector.tensor_reduce(score[:, :], prod[:, :].rearrange("p (h d) -> p h d", h=H), AX.X, ALU.add))
                    chain.step(nc.vector.tensor_scalar(score[:, :], score[:, :], float(DH) ** -0.5, None, ALU.mult))
                    nc.vector.tensor_scalar(score[:, :], score[:, :], -5.0, 5.0, ALU.max, ALU.min).then_inc(clip_ready, 1)
                    dve.wait_ge(exp_ready, k + 1)
                    nc.vector.tensor_tensor(msg[:, 0:D].rearrange("p (h d) -> p h d", h=H),
                                            rows_in[:, D:2 * D].rearrange("p (h d) -> p h d", h=H),
                                            msg[:, D:TW].unsqueeze(2).to_broadcast([P, H, DH]), ALU.mult).then_inc(msg_ready, 1)
                    dve.wait_ge(summed, k + 1)
                    nc.vector.tensor_tensor(new[:, :], bank[:, 0:TW], old[:, :], ALU.add).then_inc(new_ready, 1)
                else:
                    nc.vector.tensor_reduce(count[:, :], same[:, :], AX.X, ALU.add).then_inc(msg_ready, 1)
                    dve.wait_ge(msg_ready, k + 1)
                    dve.wait_ge(summed, k + 1)
                    dve.wait_ge(got, k * (16 * GATHERS) + 16 * GATHERS)
                    chain.step(nc.vector.tensor_reduce(part_sum[:, :], bank[:, 0:YW].rearrange("p (k d) -> p d k", k=PARTS), AX.X, ALU.add))
                    chain.step(nc.vector.tensor_tensor(new[:, 0:D], part_sum[:, :], old[:, 0:D], ALU.add))
                    nc.vector.tensor_scalar(new[:, D:TW], old[:, D:TW], count[:, :], None, ALU.add).then_inc(new_ready, 1)

            chunk(0)
            chain.loop(NCE - 1, chain.steps - 1, lambda k: chunk(k + 1))


def sum_by_edge(nc, t, v, work, bank, table, tag):
    room = Room(work, 4 * (YW + H))
    with ExitStack() as stack:
        add_by_edge(nc, t, v, room.take, stack, tag, bank, table)


def attention_by_edge(nc, t, v, work):
    with ExitStack() as ctx:
        room = Room(work)
        sums = room.take("sums", [P, 2, NP])
        with ExitStack() as edge:
            sb, ps, sem = phase(nc, edge, clear=True)
            qt, q = sb("gq_t", [P, D]), sb("gq", [P, D])
            bank, = ps("gq_bank", 1)
            ld, done, copied, st, held = (sem(f"gq_{n}") for n in ("ld", "done", "copied", "st", "held"))
            with nc.Block() as block:
                @block.sync
                def _(sp):
                    with sp.Fori(0, NT) as k:
                        sp.dma_start(qt[:, :], v.qt[:, bass.ds(k * P, P)]).then_inc(ld, 16)
                        sp.wait_ge(copied, k + 1)
                        sp.sem_inc(held, 1)
                        sp.dma_start(v.q_table[bass.ds(k * P, P), :], q[:, :]).then_inc(st, 16)
                        sp.wait_ge(st, k * 16 + 16)
                        sp.sem_inc(held, 1)

                @block.tensor
                def _(pe):
                    with pe.Fori(0, NT) as k:
                        pe.wait_ge(ld, k * 16 + 16)
                        nc.tensor.transpose(bank[:, 0:P], qt[:, :], v.ident[:, :]).then_inc(done, 1)

                @block.scalar
                def _(act):
                    with act.Fori(0, NT) as k:
                        act.wait_ge(done, k + 1)
                        nc.scalar.activation(q[:, :], bank[:, 0:P], ACT.Copy).then_inc(copied, 1)

        with ExitStack() as edge:
            bank = edge.enter_context(nc.psum_tensor("ga_bank", [P, 512], F32))
            add_by_edge(nc, t, v, room.take, edge, "_a", bank)

        with ExitStack() as edge:
            sb, ps, sem = phase(nc, edge, clear=True)
            rows_, wide = sb("gs_rows", [P, TW]), sb("gs_wide", [P, D])
            bank, = ps("gs_bank", 1)
            ld, widened, done, copied, held = (sem(f"gs_{n}") for n in ("ld", "widened", "done", "copied", "held"))
            with nc.Block() as block:
                @block.sync
                def _(sp):
                    sp.dma_start(rows_[:, :], v.totals[0:P, :]).then_inc(ld, 16)
                    with sp.Fori(1, NT) as k:
                        sp.wait_ge(copied, k)
                        sp.sem_inc(held, 1)
                        sp.dma_start(rows_[:, :], v.totals[bass.ds(k * P, P), :]).then_inc(ld, 16)

                @block.vector
                def _(dve):
                    with dve.Fori(0, NT) as k:
                        dve.wait_ge(ld, k * 16 + 16)
                        nc.vector.tensor_copy(wide[:, :].rearrange("p (h d) -> p h d", h=H),
                                              rows_[:, D:TW].unsqueeze(2).to_broadcast([P, H, DH])).then_inc(widened, 1)

                @block.tensor
                def _(pe):
                    with pe.Fori(0, NT) as k:
                        pe.wait_ge(widened, k + 1)
                        nc.tensor.transpose(bank[:, 0:P], rows_[:, 0:D], v.ident[:, :])
                        nc.tensor.transpose(bank[:, P:2 * P], wide[:, :], v.ident[:, :]).then_inc(done, 1)

                @block.scalar
                def _(act):
                    with act.Fori(0, NT) as k:
                        act.wait_ge(done, k + 1)
                        nc.scalar.activation(sums[:, :, bass.ds(k * P, P)], bank[:, 0:2 * P].rearrange("p (a n) -> p a n", a=2),
                                             ACT.Copy).then_inc(copied, 1)

        finish(nc, t, v, sums, "_by_edge")


def finish(nc, t, v, sums, tag=""):
    with ExitStack() as ctx:
        sb, ps, sem = phase(nc, ctx, tag)

        def sems(name):
            return [sem(f"{name}0"), sem(f"{name}1")]

        wo = sb("wo", [P, D])
        vectors = {n: sb(f"f_{n}", [P, D]) for n in ("bo", "gamma1", "beta1", "gamma2", "beta2")}
        inv_root = sb("f_inv_root", [P, 1])
        h_in, x_in = sb("f_h", [P, 2, D]), sb("f_x", [P, 2, D])
        attn = sb("f_attn", [P, 2, D])
        den = sb("f_den", [P, D])
        h1 = sb("f_h1", [P, D])
        h2 = sb("f_h2", [P, 2, D])
        n2 = sb("f_n2", [P, 2, D])
        n2T = sb("f_n2T", [P, 2, D])
        prod = sb("f_prod", [P, D])
        res = sb("f_res", [P, 2, D])
        stat = sb("f_stat", [P, 2, 12])
        BN, MV, VE, RSTD, NB = slice(0, 6), slice(6, 8), 8, 9, 10
        a_bank, b_bank, c_bank = ps("fa_bank", 2), ps("fb_bank", 2), ps("fc_bank", 2)
        w_in, consts = sem("f_w_in"), sem("f_consts")
        ld, st = sems("f_ld"), sems("f_st")
        attn_ready, a_done, a_read, var_ready, rstd_ready, norm2_ready, n2_ready, b_done, n2T_ready, c_done, c_read, res_ready = (
            sem(f"f_{n}") for n in ("attn_ready", "a_done", "a_read", "var_ready", "rstd_ready", "norm2_ready", "n2_ready",
                                    "b_done", "n2T_ready", "c_done", "c_read", "res_ready"))
        dve_steps, pool_steps, act_steps, sp_steps = (sem(f"f_{n}") for n in ("dve", "pool", "act", "sp"))
        held = sem("f_held")
        block = ctx.enter_context(nc.Block())

        @block.sync
        def _(sp):
            sp.dma_start(wo[:, :], t["L3_gnn_Wo"]).then_inc(w_in, 16)
            for n, tile in vectors.items():
                sp.dma_start(tile[:, :], t[f"L3_gnn_{n}"].partition_broadcast(P)).then_inc(w_in, 16)

            def load(dt):
                (dt - 1).count(sp, res_ready, held)
                sp.dma_start(h_in[:, dt.slot(), :], rows(v.h, dt)).then_inc(ld[dt.slot()], 16)
                sp.dma_start(x_in[:, dt.slot(), :], rows(v.x[2], dt)).then_inc(ld[dt.slot()], 16)

            def store(dt, n=P):
                (dt + 1).count(sp, res_ready, held)
                sp.dma_start(t["out"][bass.ds(dt.value(P), n), :], res[0:n, dt.slot(), :]).then_inc(st[dt.slot()], 16)

            def step(dt):
                load(dt)
                if dt.c >= 2:
                    store(dt - 2)

            over_tiles(Chain(sp, sp_steps), step)
            store(Num(NT - 2))
            store(Num(NT - 1), N - (NT - 1) * P)
            Num(NT - 2).landed(sp, st, held)
            Num(NT - 1).landed(sp, st, held)

        @block.gpsimd
        def _(pool):
            chain = Chain(pool, pool_steps)
            nc.gpsimd.memset(inv_root[:, :], -0.5).then_inc(consts, 1)
            pool.wait_ge(consts, 1)
            pool.wait_ge(w_in, 16 * 6)

            def step(dt):
                for i in range(2):
                    s = stat[:, i, :]
                    Num(dt.c * 2 + i + 1, dt.k, 4).count(pool, var_ready, held)
                    chain.step(nc.gpsimd.tensor_scalar(s[:, VE:VE + 1], s[:, MV.start + 1:MV.stop], EPS_LN, None, ALU.add))
                    nc.gpsimd.tensor_tensor(s[:, RSTD:RSTD + 1], s[:, VE:VE + 1], inv_root[:, :], ALU.pow).then_inc(rstd_ready, 1)
                n2_now = n2[:, dt.slot(), :]
                (dt + 1).count(pool, norm2_ready)
                chain.step(nc.gpsimd.tensor_tensor(n2_now, n2_now, vectors["gamma2"][:, :], ALU.mult))
                nc.gpsimd.tensor_tensor(n2_now, n2_now, vectors["beta2"][:, :], ALU.add).then_inc(n2_ready, 1)

            over_tiles(chain, step)

        @block.tensor
        def _(pe):
            pe.wait_ge(w_in, 16 * 6)

            def step(dt, ahead=True):
                if ahead:
                    (dt + 1).count(pe, attn_ready)
                    (dt - 1).count(pe, a_read)
                    nc.tensor.transpose(a_bank[dt.slot()][:, 0:P], attn[:, dt.slot(), :], v.ident[:, :]).then_inc(a_done, 1)
                if dt.c >= 1:
                    d = dt - 1
                    (d + 1).count(pe, n2_ready)
                    (d - 1).count(pe, n2T_ready)
                    nc.tensor.transpose(b_bank[d.slot()][:, 0:P], n2[:, d.slot(), :], v.ident[:, :]).then_inc(b_done, 1)
                    (d + 1).count(pe, n2T_ready)
                    (d - 1).count(pe, c_read)
                    nc.tensor.matmul(c_bank[d.slot()][:, 0:D], n2T[:, d.slot(), :], wo[:, :], start=True, stop=True).then_inc(c_done, 1)

            over_tiles(Chain(pe, sp_steps), step)
            step(Num(NT), ahead=False)

        @block.scalar
        def _(act):
            def step(dt):
                (dt + 1).count(act, b_done)
                (dt - 1).count(act, c_done)
                nc.scalar.activation(n2T[:, dt.slot(), :], b_bank[dt.slot()][:, 0:P], ACT.Copy).then_inc(n2T_ready, 1)

            over_tiles(Chain(act, act_steps), step)

        @block.vector
        def _(dve):
            chain = Chain(dve, dve_steps)
            dve.wait_ge(w_in, 16 * 6)

            def ratio(dt):
                at = bass.ds(dt.value(P), P)
                chain.step(nc.vector.tensor_scalar(den[:, :], sums[:, 1, at], 0.001, None, ALU.add))
                chain.step(nc.vector.reciprocal(den[:, :], den[:, :]))
                (dt - 1).count(dve, a_done)
                nc.vector.tensor_tensor(attn[:, dt.slot(), :], sums[:, 0, at], den[:, :], ALU.mult).then_inc(attn_ready, 1)

            def norm(x, dt, i, y):
                s = stat[:, i, :]
                chain.step(nc.vector.bn_stats(s[:, BN], x))
                dve.sem_inc(held, 1)
                nc.vector.bn_aggr(s[:, MV], s[:, BN]).then_inc(var_ready, 1)
                Num(dt.c * 2 + i + 1, dt.k, 4).count(dve, rstd_ready)
                return nc.vector.tensor_scalar(y, x, s[:, MV.start:MV.start + 1], s[:, RSTD:RSTD + 1], ALU.subtract, ALU.mult)

            def norms(dt):
                (dt + 1).count(dve, a_done)
                half = (dt.c // 2 + 1) * 32
                dve.wait_ge(ld[dt.slot()], half if dt.k is None else dt.k * 32 + half)
                nc.vector.tensor_tensor(h1[:, :], a_bank[dt.slot()][:, 0:P], h_in[:, dt.slot(), :], ALU.add).then_inc(a_read, 1)
                (dt + 1).count(dve, a_read)
                h2_now = h2[:, dt.slot(), :]
                chain.step(norm(h1[:, :], dt, 0, h2_now))
                chain.step(nc.vector.tensor_tensor(h2_now, h2_now, vectors["gamma1"][:, :], ALU.mult))
                chain.step(nc.vector.tensor_tensor(h2_now, h2_now, vectors["beta1"][:, :], ALU.add))
                (dt - 1).count(dve, b_done)
                norm(h2_now, dt, 1, n2[:, dt.slot(), :]).then_inc(norm2_ready, 1)

            def last(dt):
                dt.count(dve, res_ready)
                (dt + 1).count(dve, c_done)
                nc.vector.tensor_tensor(prod[:, :], c_bank[dt.slot()][:, 0:D], vectors["bo"][:, :], ALU.add).then_inc(c_read, 1)
                (dt + 1).count(dve, c_read)
                chain.step(nc.vector.scalar_tensor_tensor(prod[:, :], prod[:, :], 0.0, h2[:, dt.slot(), :], ALU.max, ALU.add))
                (dt - 2).landed(dve, st)
                nc.vector.tensor_tensor(res[:, dt.slot(), :], prod[:, :], x_in[:, dt.slot(), :], ALU.add).then_inc(res_ready, 1)

            def step(dt):
                ratio(dt)
                norms(dt)
                if dt.c >= 1:
                    last(dt - 1)

            over_tiles(chain, step)
            last(Num(NT - 1))


TRANSPOSED = ("L0_gnn_Wl1", "L0_gnn_Wr1", "L0_gnn_Wl2", "L0_gnn_Wr2", "L2_gnn_W_neigh1", "L2_gnn_W_self1",
              "L2_gnn_W_neigh2", "L2_gnn_W_self2", "L2_gnn_W_neigh3", "L2_gnn_W_self3")


def kernel(**inputs):
    import numpy as np
    import concourse.bacc as bacc
    from concourse.bass_utils import run_bass_kernel_spmd

    arrays = {}
    for name, a in inputs.items():
        a = np.asarray(a)
        if name == "x":
            a = np.pad(a, ((0, NP - N), (0, 0)))
        elif name == "src":
            a = np.pad(a, (0, NC * P - E)).reshape(NC, P).T
            name = "src_cols"
        elif name == "dst":
            arrays["dst_flat"] = np.pad(a, (0, NC * P + 2 * P - E), constant_values=PAD_DST)
            a = arrays["dst_flat"][0:NC * P]
            arrays["dst_rows"] = np.ascontiguousarray(a.reshape(P, CR * P))
            a = a.reshape(NC, P).T
            name = "dst_cols"
        elif name in TRANSPOSED:
            a = a.T
        arrays[name] = np.ascontiguousarray(a)

    nc = bacc.Bacc("TRN2", target_bir_lowering=False, num_devices=1)
    t = {n: nc.dram_tensor(f"in_{n}", a.shape, mybir.dt.from_np(a.dtype), kind="ExternalInput").ap() for n, a in arrays.items()}
    t["out"] = nc.dram_tensor("out", (N, D), F32, kind="ExternalOutput").ap()
    program(nc, t)
    r = run_bass_kernel_spmd(nc, [{f"in_{n}": a for n, a in arrays.items()}], core_ids=[0])
    return r.results[0]["out"]
```

```python
from contextlib import ExitStack

import concourse.bass as bass
from concourse import mybir

F32 = mybir.dt.float32
BF16 = mybir.dt.bfloat16
I32 = mybir.dt.int32
ALU = mybir.AluOpType
ACT = mybir.ActivationFunctionType
AX = mybir.AxisListType
ENG = mybir.EngineType

P = 128
N = 3125
E = 103125
D = 128
H = 8
DH = D // H
NT = -(-N // P)
NP = NT * P
NA = 3136
W = 8
CR = 7
NC = P * CR
WP = 12
UB = 12
TB = -(-(-(-E // P)) // (2 * UB))
GC = 4
GU = 6
CU = GC * GU
TA = -(-(-(-E // P)) // CU)
LEAD = 12
TW = D + H
NCE = -(-E // P)
DEG = 255
TURN = 4
PEELED = 5
LATE = 3
PAD_DST = 4096
PARTS = 3
YW = PARTS * D
PASSES = 7
X_IN = (0, 2, 3, 6)
X_OUT = (2, 3, 6)
S_IN = (1, 2, 3, 4, 5, 6)
NORMED = (1, 2, 3)
LAG = {0: (0, 1, 0, 2), 1: (0, 1, 0, 1), 2: (1, 2, 3, 3), 3: (1, 2, 0, 2), 4: (0, 0, 0, 1), 5: (0, 0, 0, 1), 6: (0, 1, 0, 1)}
SCALED = (2, 3)
EPS_LN = 1e-05


class Scratch:
    pass


class Num:

    def __init__(self, c, k=None, m=2):
        self.c, self.k, self.m = c, k, m

    def __add__(self, n):
        return Num(self.c + n, self.k, self.m)

    def __sub__(self, n):
        return self + -n

    def value(self, scale=1):
        return self.c * scale if self.k is None else self.k * (self.m * scale) + self.c * scale

    def slot(self, n=2):
        return self.c % n

    def count(self, engine, sem, held=None):
        if self.c > 0:
            engine.wait_ge(sem, self.value())
            if held is not None:
                engine.sem_inc(held, 1)

    def landed(self, engine, sems, held=None):
        if self.c >= 0:
            n = len(sems)
            turn = (self.c // n + 1) * 16
            engine.wait_ge(sems[self.slot(n)], turn if self.k is None else self.k * (self.m // n * 16) + turn)
            if held is not None:
                engine.sem_inc(held, 1)


class Chain:

    def __init__(self, engine, sem):
        self.engine, self.sem, self.steps, self.turned = engine, sem, 0, 0

    def start(self, ins):
        ins.then_inc(self.sem, 1)
        self.steps += 1
        return self.steps

    def wait(self, number):
        self.engine.wait_ge(self.sem, self.turned + number)

    def settle(self):
        self.engine.wait_ge(self.sem, self.turned + self.steps)

    def step(self, ins):
        self.start(ins)
        self.settle()

    def loop(self, turns, per_turn, body):
        start = self.steps
        with self.engine.Fori(0, turns) as k:
            self.turned = k * per_turn
            body(k)
            assert self.steps - start == per_turn, (self.steps - start, per_turn)
        self.turned = 0
        self.steps = start + per_turn * turns


def over_tiles(chain, step, lag):
    for dt in range(PEELED):
        before = chain.steps
        step(Num(dt))

    def body(k):
        for j in range(TURN):
            step(Num(PEELED + j, k, TURN))

    chain.loop((NT - PEELED) // TURN, (chain.steps - before) * TURN, body)
    for dt in range(NT, NT + lag):
        step(Num(dt))


def exists(dt, lag):
    assert lag < PEELED
    return dt.k is not None or 0 <= dt.c - lag < NT


def stage(do, dt, lag):
    if exists(dt, lag):
        do(dt - lag)


def nth(passes, p, dt):
    return dt + NT * passes.index(p)


def rows(tensor, dt):
    return tensor[bass.ds(dt.value(P), P), :]


ALL = tuple(range(PASSES))


def program(nc, t):
    with ExitStack() as ctx:
        def dram(name, shape, dt=F32):
            return nc.dram_tensor(name, shape, dt, kind="Internal").ap()

        v = Scratch()
        v.base = dram("window_starts", (NC,), I32)
        v.s = [dram(f"self_term{i}", (NP, D)) for i in range(2)]
        v.x = [dram(f"residual{i}", (NP, D)) for i in range(3)]
        v.h = dram("attention_input", (NP, D))
        v.kv = dram("keys_values", (NP, 2 * D))
        v.qt = dram("queries_T", (D, NP))
        v.ident = ctx.enter_context(nc.sbuf_tensor("ident", [P, P], F32))
        v.y_table = dram("y_table", (NP, YW), BF16)
        v.q_table = dram("q_table", (NP, D))
        v.totals = dram("totals", (NP, TW))
        v.odd = ctx.enter_context(nc.sbuf_tensor("odd_edges", [1, 1], I32))
        counts = ctx.enter_context(nc.sbuf_tensor("counts", [P, NT * NA + D], BF16))
        build_counts(nc, t, v, counts)
        odd = nc.values_load(v.odd[0:1, 0:1], min_val=0, max_val=1,
                             skip_runtime_bounds_check_because="a maximum of comparisons")
        with nc.If(odd < 1):
            dense_layers(nc, t, v, counts)
            attention(nc, t, v, counts)
        with nc.Else():
            dense_layers(nc, t, v, counts, by_edge=True)
            attention_by_edge(nc, t, v, counts)


class Room:

    def __init__(self, whole, start=0):
        self.whole, self.at = whole, start

    def take(self, name, shape, dt=F32):
        size = 1
        for n in shape[1:]:
            size *= n
        units = size * (1 if dt == BF16 else 2)
        piece = self.whole[0:shape[0], self.at:self.at + units]
        self.at += units + -units % 16
        assert self.at <= NT * NA + D, name
        piece = piece if dt == BF16 else piece.bitcast(dt)
        names = "abcd"[:len(shape) - 1]
        return piece.rearrange(f"p ({' '.join(names)}) -> p {' '.join(names)}", **dict(zip(names[1:], shape[2:])))


def phase(nc, stack, tag="", clear=False):
    handles = []

    def sb(name, shape, dt=F32):
        return stack.enter_context(nc.sbuf_tensor(name + tag, shape, dt))

    def ps(name, n):
        return [stack.enter_context(nc.psum_tensor(f"{name}{i}{tag}", [P, 512], F32)) for i in range(n)]

    def sem(name):
        if not clear:
            return stack.enter_context(nc.semaphore(name + tag))
        handles.append(nc.alloc_semaphore(name + tag))
        return handles[-1]

    if clear:
        def zero():
            nc.clear_and_free_semaphores(handles)
            nc.all_engine_barrier()

        stack.callback(zero)
    return sb, ps, sem


def build_counts(nc, t, v, counts):
    RH, LH = 3, 3
    KW = NT * WP
    MID = KW // 2
    with ExitStack() as ctx:
        sb, ps, sem = phase(nc, ctx, "_build", clear=True)
        dst_rows = sb("dst_rows", [P, CR, P], I32)
        dst_cols = sb("dst_cols", [P, NC], I32)
        src_cols = sb("src_cols", [P, NC], I32)
        start_f = sb("start_f", [P, CR])
        start_i = sb("start_i", [P, CR], I32)
        starts = sb("starts", [P, NC], I32)
        src_tile = sb("src_tile", [P, NC], I32)
        src_low = sb("src_low", [P, NC], I32)
        rel = sb("rel", [P, NC])
        key = sb("key", [P, NC])
        pair_rel = dst_rows[:, :, :].rearrange("p g e -> p (g e)").bitcast(F32)
        low = sb("low", [P, NC])
        iota_b = sb("iota_b", [P, KW], BF16)
        one = sb("one", [P, 1])
        right = sb("right", [P, RH, 2, KW], BF16)
        square = sb("square", [P, 3, 2, P], BF16)
        left = sb("left", [P, LH, 2, P], BF16)
        share = ps("share", 4)
        flag_bank, = ps("flag_bank", 1)
        flat = sb("flat", [P, 3, NC], I32)
        test = sb("test", [P, 2, NC], BF16)
        iota_i = test[:, 0, 0:2 * KW].bitcast(I32)
        worst = sb("worst", [P, 4])
        worst_row = src_low[0:1, 0:P].bitcast(F32)
        place = iota_b[:, MID:MID + P]

        def by_vector(q):
            return q.slot(3) == 2

        cols = counts[:, 0:NT * NA].rearrange("p (t n) -> p t n", n=NA)

        rows_in, cols_in, starts_out, starts_in = sem("rows_in"), sem("cols_in"), sem("starts_out"), sem("starts_in")
        consts, start_ready, keys_ready = sem("consts"), sem("start_ready"), sem("keys_ready")
        right_ready, mm_done, column_sums = sem("right_ready"), sem("mm_done"), sem("column_sums")
        squares_ready, left_ready = sem("squares_ready"), sem("left_ready")
        dve_steps, pool_steps = sem("dve_steps"), sem("pool_steps")
        flat_in, worst_ready, flag_done = sem("flat_in"), sem("worst_ready"), sem("flag_done")
        held = sem("held")
        block = ctx.enter_context(nc.Block())

        @block.sync
        def _(sp):
            sp.dma_start(dst_rows[:, :, :], t["dst_rows"].rearrange("p (g e) -> p g e", g=CR)).then_inc(rows_in, 16)
            sp.dma_start(dst_cols[:, :], t["dst_cols"]).then_inc(cols_in, 16)
            sp.dma_start(src_cols[:, :], t["src_cols"]).then_inc(cols_in, 16)
            for n, shift in enumerate((0, 1, DEG)):
                sp.dma_start(flat[:, n, :], t["dst_flat"][shift:shift + P * NC].rearrange("(p i) -> p i", p=P)).then_inc(flat_in, 16)
            sp.wait_ge(start_ready, 1)
            sp.dma_start(v.base.rearrange("(p g) -> p g", g=CR), start_i[:, :]).then_inc(starts_out, 16)
            sp.wait_ge(starts_out, 16)
            sp.dma_start(starts[:, :], v.base.partition_broadcast(P)).then_inc(starts_in, 16)

        @block.gpsimd
        def _(pool):
            chain = Chain(pool, pool_steps)
            chain.step(nc.gpsimd.iota(iota_i[:, :], [[1, KW]], base=-MID, channel_multiplier=0))
            chain.step(nc.gpsimd.tensor_copy(iota_b[:, :], iota_i[:, :]))
            chain.step(nc.gpsimd.memset(one[:, :], 1.0))
            chain.step(nc.gpsimd.memset(v.ident[:, :], 0.0))
            nc.gpsimd.affine_select(out=v.ident[:, :], in_=v.ident[:, :], compare_op=ALU.not_equal, fill=1.0,
                                    base=0, pattern=[[-1, P]], channel_multiplier=1).then_inc(consts, 1)
            half = (NT * NA + D) // 2
            nc.gpsimd.memset(counts[:, 0:half].bitcast(F32), 0.0).then_inc(column_sums, 1)

        @block.vector
        def _(dve):
            chain = Chain(dve, dve_steps)
            half = (NT * NA + D) // 2
            chain.step(nc.vector.memset(counts[:, half:2 * half].bitcast(F32), 0.0))
            dve.wait_ge(rows_in, 16)
            chain.step(nc.vector.tensor_reduce(start_f[:, :], dst_rows[:, :, :], AX.X, ALU.min))
            nc.vector.tensor_scalar(start_i[:, :], start_f[:, :], float(NA - WP), None, ALU.min).then_inc(start_ready, 1)
            dve.wait_ge(cols_in, 32)
            chain.step(nc.vector.tensor_scalar(src_tile[:, :], src_cols[:, :], 7, None, ALU.arith_shift_right))
            chain.step(nc.vector.tensor_scalar(src_low[:, :], src_cols[:, :], P - 1, None, ALU.bitwise_and))
            chain.step(nc.vector.tensor_copy(low[:, :], src_low[:, :]))
            dve.wait_ge(starts_in, 16)
            chain.step(nc.vector.tensor_tensor(rel[:, :], dst_cols[:, :], starts[:, :], ALU.subtract))
            pairs = [a[:, :].rearrange("p (c n) -> p c n", n=2) for a in (pair_rel, dst_cols, starts)]
            for n in range(2):
                chain.step(nc.vector.tensor_tensor(pairs[0][:, :, n:n + 1], pairs[1][:, :, n:n + 1], pairs[2][:, :, 0:1], ALU.subtract))
            chain.step(nc.vector.scalar_tensor_tensor(key[:, :], src_tile[:, :], float(WP), pair_rel[:, :], ALU.mult, ALU.add))
            nc.vector.tensor_scalar(key[:, :], key[:, :], float(-MID), None, ALU.add).then_inc(keys_ready, 1)
            dve.wait_ge(keys_ready, 1)
            dve.wait_ge(consts, 1)

            dve.wait_ge(flat_in, 48)
            here, after, far = (flat[:, n, :] for n in range(3))
            fails, more = test[:, 0, :], test[:, 1, :]
            chain.step(nc.vector.tensor_tensor(fails, after, here, ALU.is_lt))
            chain.step(nc.vector.tensor_tensor(more, far, here, ALU.is_equal))
            chain.step(nc.vector.scalar_tensor_tensor(more, here, float(PAD_DST), more, ALU.is_lt, ALU.mult))
            chain.step(nc.vector.tensor_tensor(fails, fails, more, ALU.max))
            chain.step(nc.vector.tensor_scalar(more, rel[:, :], float(W), None, ALU.is_ge))
            chain.step(nc.vector.scalar_tensor_tensor(more, dst_cols[:, :], float(PAD_DST), more, ALU.is_lt, ALU.mult))
            chain.step(nc.vector.tensor_tensor(fails, fails, more, ALU.max))
            chain.step(nc.vector.tensor_scalar(more, pair_rel[:, :], float(WP), None, ALU.is_ge))
            chain.step(nc.vector.scalar_tensor_tensor(more, dst_cols[:, :], float(PAD_DST), more, ALU.is_lt, ALU.mult))
            chain.step(nc.vector.tensor_tensor(fails, fails, more, ALU.max))
            chain.step(nc.vector.tensor_reduce(worst[:, 0:1], fails, AX.X, ALU.max))
            chain.step(nc.vector.tensor_copy(worst[:, 1:2], worst[:, 0:1]))
            nc.vector.tensor_copy(worst[:, 2:4], worst[:, 0:2]).then_inc(worst_ready, 1)
            dve.wait_ge(flag_done, 1)
            chain.step(nc.vector.tensor_copy(worst_row[:, :], flag_bank[0:1, 0:P]))
            chain.step(nc.vector.tensor_reduce(worst[0:1, 0:1], worst_row[:, :], AX.X, ALU.max))
            chain.step(nc.vector.tensor_copy(v.odd[:, :], worst[0:1, 0:1]))

            def right_sides(q):
                if by_vector(q):
                    nc.vector.tensor_scalar(left[:, q.slot(LH), 1, :], place, low[:, bass.ds(q.value(2) + 1, 1)], None, ALU.is_equal)
                for n in range(2):
                    nc.vector.tensor_scalar(right[:, q.slot(RH), n, :], iota_b[:, :], key[:, bass.ds(q.value(2) + n, 1)], None,
                                            ALU.is_equal).then_inc(right_ready, 1)

            right_sides(Num(0))
            right_sides(Num(1))
            with dve.Fori(0, TB) as k:
                _, first = nc.values_load_multi_w_load_instructions(
                    starts[0:1, bass.ds(k * (2 * UB), 2 * UB)], engines=(ENG.DVE,), min_val=0, max_val=NA - WP,
                    skip_runtime_bounds_check_because="bounded above by the min, below by the node numbers")
                for j in range(UB):
                    q = Num(j, k, UB)
                    right_sides(q + 2)
                    (q + 1).count(dve, mm_done)
                    (q + 1).count(dve, column_sums)
                    window = cols[:, :, bass.ds(first[2 * j], WP)]
                    nc.vector.tensor_tensor(window, share[j % 4][:, 0:KW].rearrange("p (t w) -> p t w", w=WP), window,
                                            ALU.add).then_inc(column_sums, 1)

        @block.scalar
        def _(act):
            act.wait_ge(consts, 1)
            act.wait_ge(keys_ready, 1)

            def squares(q):
                (q - 2).count(act, left_ready)
                sides = 1 if by_vector(q) else 2
                for n in range(sides):
                    nc.scalar.activation(square[:, q.slot(3), n, :], place, ACT.Square, bias=low[:, bass.ds(q.value(2) + n, 1)],
                                         scale=-1.0).then_inc(squares_ready, 2 // sides)

            def one_hot(q):
                act.wait_ge(squares_ready, q.value(2) + 2)
                (q - (LH - 1)).count(act, mm_done)
                sides = 1 if by_vector(q) else 2
                nc.scalar.activation(left[:, q.slot(LH), 0:sides, :], square[:, q.slot(3), 0:sides, :], ACT.Relu, bias=one[:, :],
                                     scale=-1.0).then_inc(left_ready, 1)

            def step(q):
                squares(q + 1)
                one_hot(q)

            squares(Num(0))
            for j in range(UB):
                step(Num(j))
            with act.Fori(0, TB - 1) as k:
                for j in range(UB):
                    step(Num(UB + j, k, UB))

        @block.tensor
        def _(pe):
            pe.wait_ge(consts, 1)
            pe.wait_ge(worst_ready, 1)
            nc.tensor.matmul(flag_bank[0:4, 0:P], worst[:, :], v.ident[:, :], start=True, stop=True).then_inc(flag_done, 1)
            with pe.Fori(0, TB) as k:
                for j in range(UB):
                    q = Num(j, k, UB)
                    pe.wait_ge(right_ready, q.value(2) + 2)
                    (q + 1).count(pe, left_ready)
                    for n in range(2):
                        ins = nc.tensor.matmul(share[j % 4][:, 0:KW], left[:, j % LH, n, :], right[:, j % RH, n, :],
                                               start=n == 0, stop=n == 1)
                    ins.then_inc(mm_done, 1)


def dense_layers(nc, t, v, counts, by_edge=False):
    RING = 4
    with ExitStack() as ctx:
        sb, ps, sem = phase(nc, ctx, "_by_edge" if by_edge else "", clear=by_edge)

        def sems(name, n=2):
            return [sem(f"{name}{i}") for i in range(n)]

        y3 = [sb(f"y_parts{i}", [P, NT, YW], BF16) for i in range(2)]
        weights = [sb(f"weights{i}", [P, 2 * D]) for i in range(2)]
        qt = y3[0][:, 0:2, 0:2 * D].bitcast(F32)
        wq = y3[0][:, 2, 0:2 * D].bitcast(F32)
        bq = sb("bq", [P, 1])
        bias = [sb("bias_even", [P, 2 * D]), sb("bias_odd", [P, D])]
        inv = sb("inv_count", [P, NT])
        one_col = sb("one_col", [P, 1], BF16)
        one = sb("one_f", [P, 1])
        root = sb("root", [P, 1])
        inv_root = sb("inv_root", [P, 1])
        x_in = sb("x_in", [P, RING, D])
        s_in = sb("s_in", [P, 2, D])
        s_out = sb("s_out", [P, 2, 2 * D])
        z_sum = sb("z_sum", [P, D])
        out = sb("layer_out", [P, 2, D])
        junk = sb("junk", [P, D], BF16)
        plain = sb("plain_h", [P, 2, D])
        h = sb("h", [P, 2, D])
        hT = sb("hT", [P, 2, D])
        ys = sb("ys", [P, 2, 2 * D])
        rest = sb("rest", [P, D])
        stat = sb("stat", [P, RING, 24])
        z_bank, n_bank, t_bank, d_bank = ps("z_bank", 2), ps("n_bank", 2), ps("t_bank", 2), ps("d_bank", 2)

        BN, MV, SS, FAC, CNT, SS2, NRM, CLIP, MAXN, RMAX, LOG1, LOG2, RSTD, NB, VE = (
            slice(0, 6), slice(6, 8), 8, 9, 10, 11, 12, 13, 14, 15, 16, 17, 18, 19, 20)

        w_in, w_q = sems("w_in"), sem("wq_in")
        s_ld, s_st, q_st, h_st = (sems(n) for n in ("s_ld", "s_st", "q_st", "h_st"))
        x_ld, x_st = (sems(n, RING) for n in ("x_ld", "x_st"))
        consts = sem("pass_consts")
        z_ready, z_read, out_ready, ss_ready, power_ready = (
            sem(n) for n in ("z_ready", "z_read", "out_ready", "ss_ready", "power_ready"))
        x_ready, var_ready, rstd_ready, nb_ready = (sem(n) for n in ("x_ready", "var_ready", "rstd_ready", "nb_ready"))
        ss2_ready, norm_ready, clip_ready, fn_ready, fac_ready = (
            sem(n) for n in ("ss2_ready", "norm_ready", "clip_ready", "fn_ready", "fac_ready"))
        h_ready, t_done, hT_ready, d_done, ys_ready, y_ready, s_ready = (
            sem(n) for n in ("h_ready", "t_done", "hT_ready", "d_done", "ys_ready", "y_ready", "s_ready"))
        bias_summed = sem("bias_summed")
        z_ld, z_zeroed = (sems("z_ld"), sem("z_zeroed")) if by_edge else (None, None)
        z_in = counts[:, 0:4 * (YW + H)].bitcast(F32).rearrange("p (a n) -> p a n", a=2)
        dve_steps, act_steps, pool_steps, sp_steps = (sem(n) for n in ("p_dve", "p_act", "p_pool", "p_sp"))
        held = sem("held")

        WEIGHTS = [("L0_gnn_Wl1", "L0_gnn_Wr1"), ("L0_gnn_Wl2", "L0_gnn_Wr2"), ("L1_gnn_W_neigh", "L1_gnn_W_self"),
                   ("L2_gnn_W_neigh1", "L2_gnn_W_self1"), ("L2_gnn_W_neigh2", "L2_gnn_W_self2"),
                   ("L2_gnn_W_neigh3", "L2_gnn_W_self3"), ("L3_gnn_Wk", "L3_gnn_Wv")]
        BIASES = [("L0_gnn_bl1",), ("L0_gnn_bl2",), ("L1_gnn_b_self", "L1_gnn_b_neigh"), ("L2_gnn_b_self1",),
                  ("L2_gnn_b_self2",), ("L2_gnn_b_self3",), ("L3_gnn_bk", "L3_gnn_bv")]
        loads = [16 * (2 + len(b)) for b in BIASES]

        def weights_landed(engine, p):
            engine.wait_ge(w_in[p % 2], sum(loads[p % 2:p + 1:2]))

        X_SRC = {0: t["x"], 2: t["x"], 3: v.x[0], 6: v.x[1]}

        sp_chain, pool_chain, pe_chain, act_chain, dve_chain = (
            Chain(e, m) for e, m in ((nc.sync, sp_steps), (nc.gpsimd, pool_steps), (nc.tensor, sp_steps),
                                     (nc.scalar, act_steps), (nc.vector, dve_steps)))

        def sync_passes(sp, passes):
            def load_weights(p):
                for n, name in enumerate(WEIGHTS[p]):
                    sp.dma_start(weights[p % 2][:, n * D:n * D + D], t[name]).then_inc(w_in[p % 2], 16)
                for n, name in enumerate(BIASES[p]):
                    sp.dma_start(bias[p % 2][:, n * D:n * D + D], t[name].partition_broadcast(P)).then_inc(w_in[p % 2], 16)

            def load(p, dt):
                n = nth(ALL, p, dt)
                if p in X_IN:
                    (n - (RING - 1)).count(sp, h_ready, held)
                    if p:
                        (nth(X_OUT, p, dt) - RING).landed(sp, x_st, held)
                    if p > 2:
                        nth(X_OUT, {3: 2, 6: 3}[p], dt).landed(sp, x_st, held)
                    k = nth(X_IN, p, dt)
                    sp.dma_start(x_in[:, k.slot(RING), :], rows(X_SRC[p], dt)).then_inc(x_ld[k.slot(RING)], 16)
                if p:
                    k = nth(S_IN, p, dt)
                    (k - 1).count(sp, out_ready, held)
                    nth(ALL, p - 1, dt).landed(sp, s_st, held)
                    sp.dma_start(s_in[:, k.slot(), :], rows(v.s[(p - 1) % 2], dt)).then_inc(s_ld[k.slot()], 16)
                if p and by_edge:
                    (k - 1).count(sp, z_ready, held)
                    sp.dma_start(z_in[:, k.slot(), 0:D], rows(v.totals, dt)[:, 0:D]).then_inc(z_ld[k.slot()], 16)
                    sp.dma_start(z_in[:, k.slot(), YW:YW + H], rows(v.totals, dt)[:, D:TW]).then_inc(z_ld[k.slot()], 16)

            def store_x(p, dt):
                if p in X_OUT:
                    k = nth(X_OUT, p, dt)
                    (k + 1).count(sp, x_ready, held)
                    sp.dma_start(rows(v.x[X_OUT.index(p)], dt), x_in[:, nth(X_IN, p, dt).slot(RING), :]).then_inc(x_st[k.slot(RING)], 16)

            def store_h(p, dt):
                n = nth(ALL, p, dt)
                if p == 6:
                    (n + 1).count(sp, h_ready, held)
                    sp.dma_start(rows(v.h, dt), h[:, n.slot(), :]).then_inc(h_st[dt.slot()], 16)

            def store(p, dt):
                n = nth(ALL, p, dt)
                (n + 1).count(sp, s_ready, held)
                if p < 6:
                    sp.dma_start(rows(v.s[p % 2], dt), s_out[:, n.slot(), 0:D]).then_inc(s_st[n.slot()], 16)
                else:
                    sp.dma_start(rows(v.kv, dt), s_out[:, n.slot(), :]).then_inc(s_st[n.slot()], 16)
                    (n + 1).count(sp, ys_ready, held)
                    sp.dma_start(v.qt[:, bass.ds(dt.value(P), P)], qt[:, n.slot(), :]).then_inc(q_st[dt.slot()], 16)

            if by_edge:
                sp.wait_ge(z_zeroed, passes[0] + 1)
            if 0 in passes:
                load_weights(0)
                load_weights(1)
                sp.dma_start(bq[:, :], t["L3_gnn_bq"].rearrange("(p a) -> p a", a=1)).then_inc(w_q, 16)
            for p in passes:
                if p == 6:
                    sp.wait_ge(z_ready, NT * 5)
                    sp.dma_start(wq, t["L3_gnn_Wq"]).then_inc(w_q, 16)

                if 1 <= p:
                    sp.wait_ge(d_done, NT * p)
                    sp.wait_ge(s_ready, NT * p)
                    if p < 6:
                        load_weights(p + 1)

                def step(dt):
                    stage(lambda d: load(p, d), dt, 0)
                    stage(lambda d: store_x(p, d), dt, LAG[p][0] + 1)
                    stage(lambda d: store_h(p, d), dt, LAG[p][1] + 1)
                    stage(lambda d: store(p, d), dt, min(LAG[p][3] + 2, PEELED - 1))

                over_tiles(sp_chain, step, min(LAG[p][3] + 2, PEELED - 1))
            if 6 not in passes:
                return
            for sem_, n in ((s_st, nth(ALL, 6, Num(NT - 1))), (x_st, nth(X_OUT, 6, Num(NT - 1))), (h_st, Num(NT - 1)),
                            (q_st, Num(NT - 1))):
                for back in range(len(sem_)):
                    (n - back).landed(sp, sem_, held)

        def pool_passes(pool, passes):
            chain = pool_chain
            if 0 in passes:
                chain.step(nc.gpsimd.memset(one_col[:, :], 1.0))
                chain.step(nc.gpsimd.memset(one[:, :], 1.0))
                chain.step(nc.gpsimd.memset(root[:, :], 0.5))
                nc.gpsimd.memset(inv_root[:, :], -0.5).then_inc(consts, 1)
                pool.wait_ge(consts, 1)
            if by_edge:
                chain.step(nc.gpsimd.memset(z_in[:, :, :], 0.0))
                nc.gpsimd.memset(one[:, :], 1.0).then_inc(z_zeroed, 1)
                pool.wait_ge(z_zeroed, passes[0] + 1)

            def col(n, i):
                return stat[:, n.slot(RING), i:i + 1]

            def sum_norm(p, dt):
                n = nth(ALL, p, dt)
                if p in NORMED:
                    k = nth(NORMED, p, dt)
                    (k + 1).count(pool, ss_ready, held)
                    chain.step(nc.gpsimd.tensor_scalar(col(n, SS), col(n, SS), 1e-14 if p == 3 else 1e-24, None, ALU.max))
                    nc.gpsimd.tensor_tensor(col(n, FAC), col(n, SS), (root if p == 3 else inv_root)[:, :],
                                            ALU.pow).then_inc(power_ready, 1)

            def deviation(p, dt):
                n = nth(ALL, p, dt)
                if p in X_IN:
                    k = nth(X_IN, p, dt)
                    (k + 1).count(pool, var_ready, held)
                    chain.step(nc.gpsimd.tensor_scalar(col(n, VE), col(n, MV.start + 1), EPS_LN, None, ALU.add))
                    nc.gpsimd.tensor_tensor(col(n, RSTD), col(n, VE), inv_root[:, :], ALU.pow).then_inc(rstd_ready, 1)

            def h_norm(p, dt):
                n = nth(ALL, p, dt)
                if p == 2:
                    (dt + 1).count(pool, ss2_ready)
                    nc.gpsimd.tensor_tensor(col(n, NRM), col(n, SS2), root[:, :], ALU.pow).then_inc(norm_ready, 1)

            def self_term(p, dt):
                n = nth(ALL, p, dt)
                (n + 1).count(pool, ys_ready)
                (n - 2).landed(pool, s_st)
                a, b = (0, 2 * D) if p == 6 else (D, 2 * D)
                nc.gpsimd.tensor_tensor(s_out[:, n.slot(), 0:b - a], ys[:, n.slot(), a:b], bias[p % 2][:, 0:b - a],
                                        ALU.add).then_inc(s_ready, 1)

            for p in passes:
                weights_landed(pool, p)
                if p == 2:
                    nc.gpsimd.tensor_tensor(bias[0][:, 0:D], bias[0][:, 0:D], bias[0][:, D:2 * D], ALU.add).then_inc(bias_summed, 1)
                    pool.wait_ge(bias_summed, 1)

                def step(dt):
                    new_x, norm, _, last = LAG[p]
                    stage(lambda d: h_norm(p, d), dt, norm)
                    stage(lambda d: deviation(p, d), dt, new_x)
                    stage(lambda d: sum_norm(p, d), dt, 0)
                    stage(lambda d: self_term(p, d), dt, last + 1)

                over_tiles(chain, step, LAG[p][3] + 1)

        def tensor_passes(pe, passes):
            chain = pe_chain
            pe.wait_ge(consts, 1)

            def transpose(p, dt):
                n = nth(ALL, p, dt)
                (n + 1).count(pe, h_ready)
                (n - 1).count(pe, hT_ready)
                nc.tensor.transpose(t_bank[n.slot()][:, 0:P], h[:, n.slot(), :], v.ident[:, :]).then_inc(t_done, 1)

            def products(p, dt):
                n = nth(ALL, p, dt)
                (n + 1).count(pe, hT_ready)
                (n - 1).count(pe, ys_ready)
                out_ = d_bank[n.slot()]
                ins = nc.tensor.matmul(out_[:, 0:2 * D], hT[:, n.slot(), :], weights[p % 2][:, :], start=True, stop=True)
                if p == 6:
                    ins = nc.tensor.matmul(out_[:, 2 * D:3 * D], wq, hT[:, n.slot(), :], start=True, stop=True)
                ins.then_inc(d_done, 1)

            def neighbour_sum(p, dt):
                k = nth(S_IN, p, dt)
                (k - 1).count(pe, z_read)
                if by_edge:
                    half = (k.c // 2 + 1) * 32
                    pe.wait_ge(z_ld[k.slot()], half if k.k is None else k.k * (k.m // 2 * 32) + half)
                    ins = nc.tensor.matmul(z_bank[k.slot()][:, 0:YW], v.ident[:, :], z_in[:, k.slot(), 0:YW], start=True, stop=True)
                    if p == 1:
                        ins = nc.tensor.matmul(n_bank[k.slot()][:, 0:1], v.ident[:, :], z_in[:, k.slot(), YW:YW + 1],
                                               start=True, stop=True)
                    ins.then_inc(z_ready, 1)
                    stage(lambda d: transpose(p, d), dt, LAG[p][3])
                    return
                for s in range(NT):
                    if dt.k is None and dt.c == 0:
                        if s == 0:
                            pe.wait_ge(y_ready, NT * p - LATE)
                        if s == NT - LATE:
                            pe.wait_ge(y_ready, NT * p)
                    lhs = counts[:, bass.ds(dt.value(P) + s * NA, P)]
                    ins = nc.tensor.matmul(z_bank[k.slot()][:, 0:YW], lhs, y3[(p - 1) % 2][:, s, :],
                                           start=s == 0, stop=s == NT - 1)
                    if p == 1:
                        ins = nc.tensor.matmul(n_bank[k.slot()][:, 0:1], lhs, one_col[:, :],
                                               start=s == 0, stop=s == NT - 1)
                    if s == NT - 1:
                        ins.then_inc(z_ready, 1)
                    if s == (22 if p == 2 else 17):
                        stage(lambda d: transpose(p, d), dt, LAG[p][3])

            for p in passes:
                weights_landed(pe, p)
                if p == 6:
                    pe.wait_ge(w_q, 32)

                def step(dt):
                    if p and (dt.k is not None or dt.c < NT):
                        neighbour_sum(p, dt)
                    else:
                        stage(lambda d: transpose(p, d), dt, LAG[p][3])
                    stage(lambda d: products(p, d), dt, LAG[p][3])

                over_tiles(chain, step, LAG[p][3])

        def scalar_passes(act, passes):
            chain = act_chain
            act.wait_ge(consts, 1)

            def col(n, i):
                return stat[:, n.slot(RING), i:i + 1]

            def second(p, dt):
                n = nth(ALL, p, dt)
                (n + 1).count(act, t_done)
                (n - 1).count(act, d_done)
                nc.scalar.activation(hT[:, n.slot(), :], t_bank[n.slot()][:, 0:P], ACT.Copy).then_inc(hT_ready, 1)
                (n + 1).count(act, d_done)
                (n - 1).count(act, s_ready)
                if p < 6:
                    (n - 1).count(act, y_ready)
                    chain.step(nc.scalar.activation(ys[:, n.slot(), :], d_bank[n.slot()][:, 0:2 * D], ACT.Copy))
                    nc.scalar.activation(y3[p % 2][:, bass.ds(dt.value(), 1), 0:D].rearrange("p a d -> p (a d)"),
                                         ys[:, n.slot(), 0:D], ACT.Copy).then_inc(ys_ready, 1)
                else:
                    (dt - 2).landed(act, q_st)
                    chain.step(nc.scalar.activation(ys[:, n.slot(), :], d_bank[n.slot()][:, 0:2 * D], ACT.Copy))
                    nc.scalar.activation(qt[:, n.slot(), :], d_bank[n.slot()][:, 2 * D:3 * D], ACT.Identity,
                                         bias=bq[:, :]).then_inc(ys_ready, 1)

            def sum_squares(p, dt):
                n = nth(ALL, p, dt)
                if p in NORMED:
                    k = nth(S_IN, p, dt)
                    (k + 1).count(act, out_ready)
                    nc.scalar.activation(junk[:, :], out[:, n.slot(), :], ACT.Square, accum_out=col(n, SS)).then_inc(ss_ready, 1)
                    (nth(NORMED, p, dt) + 1).count(act, ss_ready)

            def tanh(p, dt):
                n = nth(ALL, p, dt)
                if p == 3:
                    (nth(SCALED, p, dt) + 1).count(act, clip_ready)
                    nc.scalar.activation(col(n, LOG1), col(n, CLIP), ACT.Tanh).then_inc(fn_ready, 1)

            def next_h(p, dt):
                n = nth(ALL, p, dt)
                (n - 1).count(act, t_done)
                if p == 6:
                    (dt - 2).landed(act, h_st)
                if p == 2:
                    (n - 1).count(act, h_ready)
                h_out = h[:, n.slot(), :]
                if p == 1:
                    (nth(NORMED, p, dt) + 1).count(act, power_ready)
                    nc.scalar.activation(h_out, out[:, n.slot(), :], ACT.Relu, scale=col(n, FAC)).then_inc(h_ready, 1)
                if p in (4, 5):
                    (nth(S_IN, p, dt) + 1).count(act, out_ready)
                    nc.scalar.activation(h_out, out[:, n.slot(), :], ACT.Relu).then_inc(h_ready, 1)
                if p in X_IN:
                    k = nth(X_IN, p, dt)
                    (k + 1).count(act, nb_ready)
                    x_now = x_in[:, k.slot(RING), :]
                    ins = nc.scalar.activation(plain[:, n.slot(), :] if p == 2 else h_out, x_now, ACT.Relu, bias=col(n, NB),
                                               scale=col(n, RSTD))
                    if p != 2:
                        ins.then_inc(h_ready, 1)
                    else:
                        chain.step(ins)
                        nc.scalar.activation(junk[:, :], plain[:, n.slot(), :], ACT.Square, accum_out=col(n, SS2)).then_inc(ss2_ready, 1)
                        (dt + 1).count(act, ss2_ready)

            def logs(p, dt):
                n = nth(ALL, p, dt)
                if p == 2:
                    (nth(SCALED, p, dt) + 1).count(act, clip_ready)
                    chain.step(nc.scalar.activation(col(n, LOG1), col(n, CLIP), ACT.Ln, bias=one[:, :]))
                    nc.scalar.activation(col(n, LOG2), col(n, CLIP), ACT.Ln, bias=one[:, :], scale=-1.0).then_inc(fn_ready, 1)

            def log_map(p, dt):
                n = nth(ALL, p, dt)
                h_out = h[:, n.slot(), :]
                if p == 2:
                    (dt + 1).count(act, fac_ready)
                    nc.scalar.activation(h_out, plain[:, n.slot(), :], ACT.Copy, scale=col(n, FAC)).then_inc(h_ready, 1)

            for p in passes:
                if p == 6:
                    act.wait_ge(w_q, 32)

                def step(dt):
                    new_x, norm, log, last = LAG[p]
                    stage(lambda d: logs(p, d), dt, log)
                    if norm:
                        stage(lambda d: next_h(p, d), dt, norm)
                    stage(lambda d: log_map(p, d), dt, log)
                    stage(lambda d: tanh(p, d), dt, new_x)
                    stage(lambda d: second(p, d), dt, last)
                    stage(lambda d: sum_squares(p, d), dt, 0)
                    if not norm:
                        stage(lambda d: next_h(p, d), dt, norm)

                over_tiles(chain, step, LAG[p][3])

        def vector_passes(dve, passes):
            chain = dve_chain

            def col(n, i):
                return stat[:, n.slot(RING), i:i + 1]

            def new_out(p, dt):
                n = nth(ALL, p, dt)
                this = out[:, n.slot(), :]
                if p:
                    k = nth(S_IN, p, dt)
                    z = z_bank[k.slot()]
                    k.count(dve, out_ready)
                    (k + 1).count(dve, z_ready)
                    inv_now = inv[:, bass.ds(dt.value(), 1)]
                    if p == 1:
                        chain.step(nc.vector.tensor_scalar(col(n, CNT), n_bank[k.slot()][:, 0:1], 1.0, None, ALU.max))
                        chain.step(nc.vector.reciprocal(inv_now, col(n, CNT)))
                    nc.vector.tensor_reduce(z_sum[:, :], z[:, 0:YW].rearrange("p (k d) -> p d k", k=PARTS), AX.X,
                                            ALU.add).then_inc(z_read, 1)
                    (k + 1).count(dve, z_read)
                    k.landed(dve, s_ld)
                    if p in (1, 4, 5):
                        (n - 1).count(dve, h_ready)
                    nc.vector.scalar_tensor_tensor(this, z_sum[:, :], inv_now, s_in[:, k.slot(), :], ALU.mult,
                                                   ALU.add).then_inc(out_ready, 1)

            def new_x(p, dt):
                n = nth(ALL, p, dt)
                this = out[:, n.slot(), :]
                if p not in X_IN:
                    return
                k = nth(X_IN, p, dt)
                x_now = x_in[:, k.slot(RING), :]
                if p:
                    kx = nth(X_OUT, p, dt)
                    if p in NORMED:
                        (nth(NORMED, p, dt) + 1).count(dve, power_ready)
                    if p == 3:
                        nc.vector.tensor_scalar(col(n, CLIP), col(n, FAC), 15.0, None, ALU.min).then_inc(clip_ready, 1)
                        chain.step(nc.vector.reciprocal(col(n, RMAX), col(n, FAC)))
                        (nth(SCALED, p, dt) + 1).count(dve, fn_ready)
                        chain.step(nc.vector.tensor_tensor(col(n, FAC), col(n, LOG1), col(n, RMAX), ALU.mult))
                    if p == 6:
                        (nth(S_IN, p, dt) + 1).count(dve, out_ready)
                    k.landed(dve, x_ld)
                    if p == 6:
                        nc.vector.tensor_tensor(x_now, this, x_now, ALU.add).then_inc(x_ready, 1)
                    else:
                        nc.vector.scalar_tensor_tensor(x_now, this, col(n, FAC), x_now, ALU.mult, ALU.add).then_inc(x_ready, 1)
                    (kx + 1).count(dve, x_ready)
                else:
                    k.landed(dve, x_ld)
                chain.step(nc.vector.bn_stats(stat[:, n.slot(RING), BN], x_now))
                dve.sem_inc(held, 1)
                nc.vector.bn_aggr(stat[:, n.slot(RING), MV], stat[:, n.slot(RING), BN]).then_inc(var_ready, 1)

            def norm_bias(p, dt):
                if p not in X_IN:
                    return
                n = nth(ALL, p, dt)
                (nth(X_IN, p, dt) + 1).count(dve, rstd_ready)
                nc.vector.tensor_scalar(col(n, NB), col(n, MV.start), col(n, RSTD), -1.0, ALU.mult, ALU.mult).then_inc(nb_ready, 1)

            def log_argument(p, dt):
                n = nth(ALL, p, dt)
                if p == 2:
                    (dt + 1).count(dve, norm_ready)
                    nc.vector.tensor_scalar(col(n, CLIP), col(n, NRM), 1e-7, 1.0 - 1e-5, ALU.max, ALU.min).then_inc(clip_ready, 1)
                    chain.step(nc.vector.tensor_scalar(col(n, MAXN), col(n, NRM), 1e-7, None, ALU.max))
                    chain.step(nc.vector.reciprocal(col(n, RMAX), col(n, MAXN)))

            def log_factor(p, dt):
                n = nth(ALL, p, dt)
                if p == 2:
                    (nth(SCALED, p, dt) + 1).count(dve, fn_ready)
                    chain.step(nc.vector.tensor_tensor(col(n, LOG1), col(n, LOG1), col(n, LOG2), ALU.subtract))
                    nc.vector.tensor_scalar(col(n, FAC), col(n, LOG1), 0.5, col(n, RMAX), ALU.mult, ALU.mult).then_inc(fac_ready, 1)

            def second(p, dt):
                n = nth(ALL, p, dt)
                nth(ALL, p, dt).count(dve, y_ready)
                (n + 1).count(dve, ys_ready)
                part = [y3[p % 2][:, bass.ds(dt.value(), 1), i * D:i * D + D].rearrange("p a d -> p (a d)") for i in range(PARTS)]
                chain.step(nc.vector.tensor_tensor(rest[:, :], ys[:, n.slot(), 0:D], part[0], ALU.subtract))
                chain.step(nc.vector.tensor_copy(part[1], rest[:, :]))
                nc.vector.tensor_tensor(part[2], rest[:, :], part[1], ALU.subtract).then_inc(y_ready, 1)

            for p in passes:
                def step(dt):
                    x, norm, log, last = LAG[p]
                    stage(lambda d: log_argument(p, d), dt, log)
                    if norm > x:
                        stage(lambda d: norm_bias(p, d), dt, norm)
                    if x:
                        stage(lambda d: new_x(p, d), dt, x)
                    stage(lambda d: log_factor(p, d), dt, log)
                    stage(lambda d: new_out(p, d), dt, 0)
                    if not x:
                        stage(lambda d: new_x(p, d), dt, x)
                    if p < 6:
                        stage(lambda d: second(p, d), dt, last + 1)

                over_tiles(chain, step, LAG[p][3] + 1)

        def run(passes):
            with nc.Block() as block:
                block.sync(lambda sp: sync_passes(sp, passes))
                block.gpsimd(lambda pool: pool_passes(pool, passes))
                block.tensor(lambda pe: tensor_passes(pe, passes))
                block.scalar(lambda act: scalar_passes(act, passes))
                block.vector(lambda dve: vector_passes(dve, passes))

        if not by_edge:
            run(ALL)
            return
        for p in ALL:
            if p:
                sum_by_edge(nc, t, v, counts, z_bank[0], y3[(p - 1) % 2], f"_{p}")
            run((p,))


def attention(nc, t, v, counts):
    GW = GC * W * H
    LAST = GU * TA
    with ExitStack() as ctx:
        room = Room(counts)
        sums = room.take("sums", [P, 2, NP])
        with ExitStack() as edge:
            sb, ps, sem = phase(nc, edge)
            queries = room.take("queries", [P, NP, H])
            qt = sb("qt_all", [P, NP])
            head, head_scale = sb("head", [P, H]), sb("head_scale", [P, H])
            src_cols = sb("a_src", [P, NC], I32)
            dst_cols = sb("a_dst", [P, NC], I32)
            starts = sb("a_starts", [P, LEAD + NC], I32)
            rel = sb("a_rel", [P, NC])
            iota_i = sb("a_iota_i", [P, W], I32)
            iota_f = sb("a_iota", [P, W])
            ones = sb("a_ones", [P, P])
            index = sb("index", [P, GU, GC], I32)
            rows_kv = room.take("rows_kv", [P, GU, GC, 2 * D])
            kT = sb("kT", [P, 2, GC * P])
            clipped = sb("clipped", [P, 2, GW])
            weight = sb("weight", [P, 2, GW])
            masked = sb("masked", [P, 2, GW])
            here = sb("here", [P, 2, GC, W])
            picked = sb("picked", [P, 2 * GC * W, H])
            added = sb("added", [P, 2 * GC * W])
            t_bank, s_bank, o_bank = ps("at_bank", 2), ps("as_bank", 2), ps("ao_bank", 2)

            ld = [sem(f"a_ld{i}") for i in range(4)]
            gathered = [sem(f"gathered{i}") for i in range(GU)]
            consts, rel_ready = sem("a_consts"), sem("rel_ready")
            queries_act, queries_dve = sem("queries_act"), sem("queries_dve")
            t_done, kT_ready, s_done, clip_done, exp_done = (sem(n) for n in ("at_done", "kT_ready", "as_done", "clip_done", "exp_done"))
            masked_ready, o_done, picked_ready, index_ready = (sem(n) for n in ("masked_ready", "o_done", "picked_ready", "index_ready"))
            dve_steps, pool_steps = sem("a_dve"), sem("a_pool")
            held = sem("a_held")
            block = edge.enter_context(nc.Block())

            def spread_queries(compute, heads, ready):
                for n in heads:
                    compute(queries[:, :, n:n + 1].rearrange("p n a -> p (n a)"), qt[:, :],
                            head_scale[:, n:n + 1]).then_inc(ready, 1)

            def groups(engine, per_group, chain=None):
                for j in range(GU):
                    per_group(Num(j, None, GU), j)

                def body(k):
                    for j in range(GU):
                        per_group(Num(GU + j, k, GU), j)

                return body

            def first_nodes(engine_type, first_group, k):
                at = k * CU + (LEAD + first_group * GC) if k is not None else LEAD + first_group * GC
                _, regs = nc.values_load_multi_w_load_instructions(
                    starts[0:1, bass.ds(at, CU)], engines=(engine_type,), min_val=0, max_val=NA - WP,
                    skip_runtime_bounds_check_because="bounded by the build")
                return regs

            @block.sync
            def _(sp):
                sp.dma_start(src_cols[:, :], t["src_cols"]).then_inc(ld[0], 16)
                sp.dma_start(dst_cols[:, :], t["dst_cols"]).then_inc(ld[1], 16)
                sp.dma_start(starts[:, LEAD:], v.base.partition_broadcast(P)).then_inc(ld[2], 16)
                sp.dma_start(qt[:, :], v.qt).then_inc(ld[3], 16)

            @block.gpsimd
            def _(pool):
                chain = Chain(pool, pool_steps)
                chain.step(nc.gpsimd.memset(head[:, :], 1.0))
                chain.step(nc.gpsimd.affine_select(out=head[:, :], in_=head[:, :], compare_op=ALU.is_ge, fill=0.0,
                                                   base=0, pattern=[[-DH, H]], channel_multiplier=1))
                chain.step(nc.gpsimd.affine_select(out=head[:, :], in_=head[:, :], compare_op=ALU.is_ge, fill=0.0,
                                                   base=DH - 1, pattern=[[DH, H]], channel_multiplier=-1))
                chain.step(nc.gpsimd.tensor_scalar(head_scale[:, :], head[:, :], float(DH) ** -0.5, None, ALU.mult))
                chain.step(nc.gpsimd.iota(iota_i[:, :], [[1, W]], base=0, channel_multiplier=0))
                chain.step(nc.gpsimd.tensor_copy(iota_f[:, :], iota_i[:, :]))
                chain.step(nc.gpsimd.memset(ones[:, :], 1.0))
                chain.step(nc.gpsimd.memset(starts[:, 0:LEAD], 0))
                nc.gpsimd.memset(sums[:, :, :], 0.0).then_inc(consts, 1)

                def gather(g, j):
                    (g + 1).count(pool, index_ready, held)
                    (g - (GU - 1)).count(pool, o_done, held)
                    for c in range(GC):
                        nc.gpsimd.indirect_dma_start(rows_kv[:, j, c, :], None, v.kv,
                                                     bass.IndirectOffsetOnAxis(index[:, j, c:c + 1], 0)).then_inc(gathered[j], 16)

                body = groups(pool, gather)
                with pool.Fori(0, TA - 1) as k:
                    body(k)

            @block.scalar
            def _(act):
                act.wait_ge(ld[0], 16)
                act.wait_ge(consts, 1)

                def stage_index(g, j):
                    nc.scalar.activation(index[:, j, :], src_cols[:, bass.ds(g.value(GC), GC)], ACT.Copy).then_inc(index_ready, 1)

                for j in range(GU - 1):
                    stage_index(Num(j), j)

                act.wait_ge(ld[3], 16)
                spread_queries(lambda y, x, scale: nc.scalar.activation(y, x, ACT.Copy, scale=scale), range(H // 2, H), queries_act)

                def step(g, j, load=True, copy=True):
                    if copy:
                        (g + 1).count(act, t_done)
                        (g - 1).count(act, s_done)
                        nc.scalar.activation(kT[:, g.slot(), :], t_bank[g.slot()][:, :], ACT.Copy).then_inc(kT_ready, 1)
                    if load:
                        stage_index(g + (GU - 1), (j - 1) % GU)
                    if g.c >= 1:
                        g.count(act, clip_done)
                        (g - 2).count(act, masked_ready)
                        nc.scalar.activation(weight[:, (g - 1).slot(), :], clipped[:, (g - 1).slot(), :], ACT.Exp).then_inc(exp_done, 1)

                body = groups(act, step)
                if TA > 2:
                    with act.Fori(0, TA - 2) as k:
                        body(k)
                for j in range(GU):
                    step(Num(LAST - GU + j), j, load=j == 0)
                step(Num(LAST), 0, load=False, copy=False)

            @block.tensor
            def _(pe):
                pe.wait_ge(consts, 1)
                pe.wait_ge(queries_act, H - H // 2)
                pe.wait_ge(queries_dve, H // 2)
                pe.wait_ge(ld[2], 16)

                def step(g, j, regs, copy=True):
                    if copy:
                        turn = g.c // GU + 1
                        pe.wait_ge(gathered[j], turn * 16 * GC if g.k is None else g.k * (16 * GC) + turn * 16 * GC)
                        (g - 1).count(pe, kT_ready)
                        for c in range(GC):
                            ins = nc.tensor.transpose(t_bank[g.slot()][:, c * P:c * P + P], rows_kv[:, j, c, 0:D], v.ident[:, :])
                        ins.then_inc(t_done, 1)
                    if g.c >= 1 and g.c - 1 < LAST:
                        g1 = g - 1
                        g.count(pe, kT_ready)
                        (g1 - 1).count(pe, clip_done)
                        for c in range(GC):
                            ins = nc.tensor.matmul(s_bank[g1.slot()][:, c * W * H:(c + 1) * W * H],
                                                   kT[:, g1.slot(), c * P:c * P + P],
                                                   queries[:, bass.ds(regs[j * GC + c], W), :].rearrange("p w h -> p (w h)"),
                                                   start=True, stop=True)
                        ins.then_inc(s_done, 1)
                    if g.c >= 2:
                        g2 = g - 2
                        (g2 + 1).count(pe, masked_ready)
                        (g2 - 1).count(pe, picked_ready)
                        for c in range(GC):
                            nc.tensor.matmul(o_bank[g2.slot()][:, c * W * H:(c + 1) * W * H], rows_kv[:, (j - 2) % GU, c, D:2 * D],
                                             masked[:, g2.slot(), c * W * H:(c + 1) * W * H], start=True, stop=True)
                        nc.tensor.matmul(o_bank[g2.slot()][:, GW:2 * GW], ones[:, :], masked[:, g2.slot(), :],
                                         start=True, stop=True).then_inc(o_done, 1)

                regs = first_nodes(ENG.PE, -1, None)
                for j in range(GU):
                    step(Num(j), j, regs)
                with pe.Fori(0, TA - 1) as k:
                    regs = first_nodes(ENG.PE, GU - 1, k)
                    for j in range(GU):
                        step(Num(GU + j, k, GU), j, regs)
                regs = first_nodes(ENG.PE, LAST - 1, None)
                for j in range(2):
                    step(Num(LAST + j), j, regs, copy=False)

            @block.vector
            def _(dve):
                chain = Chain(dve, dve_steps)
                dve.wait_ge(consts, 1)
                dve.wait_ge(ld[1], 16)
                dve.wait_ge(ld[2], 16)
                nc.vector.tensor_tensor(rel[:, :], dst_cols[:, :], starts[:, LEAD:], ALU.subtract).then_inc(rel_ready, 1)
                dve.wait_ge(rel_ready, 1)
                dve.wait_ge(ld[3], 16)
                spread_queries(lambda y, x, scale: nc.vector.tensor_scalar(y, x, scale, None, ALU.mult), range(H // 2), queries_dve)

                def step(g, j, regs):
                    g1, g3 = g - 1, g - 3
                    ahead, behind = 1 <= g.c <= LAST, g.c >= 3
                    if behind:
                        (g3 + 1).count(dve, o_done)
                        nc.vector.tensor_tensor(picked[:, :, :], o_bank[g3.slot()][:, :].rearrange("p (n h) -> p n h", h=H),
                                                head[:, :].unsqueeze(1).to_broadcast([P, 2 * GC * W, H]),
                                                ALU.mult).then_inc(picked_ready, 1)
                    if ahead:
                        chain.start(nc.vector.tensor_tensor(
                            here[:, g1.slot(), :, :], rel[:, bass.ds(g1.value(GC), GC)].unsqueeze(2).to_broadcast([P, GC, W]),
                            iota_f[:, :].unsqueeze(1).to_broadcast([P, GC, W]), ALU.is_equal))
                        g.count(dve, s_done)
                        nc.vector.tensor_scalar(clipped[:, g1.slot(), :], s_bank[g1.slot()][:, 0:GW], -5.0, 5.0, ALU.max,
                                                ALU.min).then_inc(clip_done, 1)

                    def add(c):
                        parts = added[:, :].rearrange("p (a c w) -> p a c w", a=2, c=GC)
                        window = sums[:, :, bass.ds(regs[j * GC + c], W)]
                        chain.start(nc.vector.tensor_tensor(window, window, parts[:, :, c, :], ALU.add))

                    if behind:
                        (g3 + 1).count(dve, picked_ready)
                        chain.step(nc.vector.tensor_reduce(added[:, :], picked[:, :, :], AX.X, ALU.add))
                        add(0)
                    if ahead or behind:
                        chain.settle()
                    if ahead:
                        g.count(dve, exp_done)
                        (g1 - 1).count(dve, o_done)
                        nc.vector.tensor_tensor(masked[:, g1.slot(), :].rearrange("p (n h) -> p n h", h=H),
                                                weight[:, g1.slot(), :].rearrange("p (n h) -> p n h", h=H),
                                                here[:, g1.slot(), :, :].rearrange("p c w -> p (c w)").unsqueeze(2).to_broadcast([P, GC * W, H]),
                                                ALU.mult).then_inc(masked_ready, 1)
                    if behind:
                        for c in range(1, GC):
                            add(c)
                            chain.settle()

                regs = first_nodes(ENG.DVE, -3, None)
                for j in range(GU):
                    step(Num(j), j, regs)

                def turn(k):
                    regs = first_nodes(ENG.DVE, GU - 3, k)
                    for j in range(GU):
                        step(Num(GU + j, k, GU), j, regs)

                chain.loop(TA - 1, GU * (2 + GC), turn)
                regs = first_nodes(ENG.DVE, LAST - 3, None)
                for j in range(3):
                    step(Num(LAST + j), j, regs)

        finish(nc, t, v, sums)


def add_by_edge(nc, t, v, sb, stack, tag, bank, table=None):
    attend = table is None

    _, _, sem = phase(nc, stack, f"_ge{tag}", clear=True)

    width = 2 * D if attend else YW
    dt = F32 if attend else BF16
    src_cols, dst_cols, low_cols = sb("src", [P, NC], I32), sb("dst", [P, NC], I32), sb("low", [P, NC], I32)
    dst_f = sb("dst_f", [P, NC])
    lower = sb("lower", [P, P])
    ones = sb("ones", [P, P])
    zeros = sb("zeros", [P, NT, TW])
    index = sb("index", [P, 2], I32)
    rows_in = sb("rows", [P, width], dt)
    old, new = sb("old", [P, TW]), sb("new", [P, TW])
    dst_row = sb("dst_row", [P, P], I32)
    same, before = sb("same", [P, P], dt), sb("before", [P, P])
    dup, count = sb("dup", [P, 1]), sb("count", [P, 1])
    target = sb("target", [P, 1], I32)
    part_sum = sb("part_sum", [P, D])
    q_rows, prod, score = sb("q_rows", [P, D]), sb("prod", [P, D]), sb("score", [P, H])
    msg = sb("msg", [P, TW])
    cols_in, consts, low_ready, zeroed, tables_ready, landed, row_in, staged = (sem(n) for n in ("cols_in", "consts", "low_ready", "zeroed", "tables_ready", "landed", "row_in", "staged"))
    got, clip_ready, exp_ready, msg_ready = (sem(n) for n in ("got", "clip", "exp", "msg"))
    summed, new_ready, dve_steps, pool_steps, held = (sem(n) for n in ("summed", "new", "dve", "pool", "held"))
    GATHERS = 3 if attend else 2

    def over_chunks(engine, body):
        body(0)
        with engine.Fori(0, NCE - 1) as k:
            body(k + 1)

    def chunk_before(engine, k):
        if not isinstance(k, int):
            engine.wait_ge(landed, k * 16)

    with nc.Block() as block:
        @block.sync
        def _(sp):
            sp.dma_start(src_cols[:, :], t["src_cols"]).then_inc(cols_in, 16)
            sp.dma_start(dst_cols[:, :], t["dst_cols"]).then_inc(cols_in, 16)
            sp.wait_ge(consts, 1)
            sp.dma_start(v.totals.rearrange("(t p) c -> p t c", p=P), zeros[:, :, :]).then_inc(zeroed, 16)
            if table is not None:
                sp.dma_start(v.y_table.rearrange("(t p) c -> p t c", p=P), table[:, :, :]).then_inc(zeroed, 16)
            sp.wait_ge(zeroed, 16 if attend else 32)
            sp.sem_inc(tables_ready, 1)

            def chunk(k):
                chunk_before(sp, k)
                sp.sem_inc(held, 1)
                sp.dma_start(dst_row[:, :], t["dst_flat"][bass.ds(k * P, P)].partition_broadcast(P)).then_inc(row_in, 16)

            over_chunks(sp, chunk)
            sp.wait_ge(landed, NCE * 16)

        @block.gpsimd
        def _(pool):
            chain = Chain(pool, pool_steps)
            chain.step(nc.gpsimd.memset(zeros[:, :, :], 0.0))
            chain.step(nc.gpsimd.memset(ones[:, :], 1.0))
            chain.step(nc.gpsimd.memset(old[:, :], 0.0))
            nc.gpsimd.affine_select(out=lower[:, :], in_=ones[:, :], compare_op=ALU.is_gt, fill=0.0, base=0,
                                    pattern=[[-1, P]], channel_multiplier=1).then_inc(consts, 1)
            pool.wait_ge(tables_ready, 1)

            def chunk(k):
                pool.wait_ge(staged, k + 1)
                pool.sem_inc(held, 1)
                nc.gpsimd.indirect_dma_start(rows_in[:, :], None, v.kv if attend else v.y_table,
                                             bass.IndirectOffsetOnAxis(index[:, 0:1], 0)).then_inc(got, 16)
                nc.gpsimd.indirect_dma_start(old[:, :], None, v.totals, bass.IndirectOffsetOnAxis(index[:, 1:2], 0)).then_inc(got, 16)
                if attend:
                    nc.gpsimd.indirect_dma_start(q_rows[:, :], None, v.q_table,
                                                 bass.IndirectOffsetOnAxis(index[:, 1:2], 0)).then_inc(got, 16)
                pool.wait_ge(new_ready, k + 1)
                pool.sem_inc(held, 1)
                nc.gpsimd.indirect_dma_start(v.totals, bass.IndirectOffsetOnAxis(target[:, :], 0), new[:, :], None,
                                             bounds_check=NP - 1, oob_is_err=False).then_inc(landed, 16)

            over_chunks(pool, chunk)

        @block.scalar
        def _(act):
            act.wait_ge(cols_in, 32)
            act.wait_ge(low_ready, 1)

            def chunk(k):
                chunk_before(act, k)
                nc.scalar.activation(index[:, 0:1], src_cols[:, bass.ds(k, 1)], ACT.Copy).then_inc(held, 1)
                nc.scalar.activation(index[:, 1:2], low_cols[:, bass.ds(k, 1)], ACT.Copy).then_inc(staged, 1)
                if attend:
                    act.wait_ge(clip_ready, k + 1)
                    nc.scalar.activation(msg[:, D:TW], score[:, :], ACT.Exp).then_inc(exp_ready, 1)

            over_chunks(act, chunk)

        @block.tensor
        def _(pe):
            def chunk(k):
                pe.wait_ge(msg_ready, k + 1)
                pe.wait_ge(got, k * (16 * GATHERS) + 16 * GATHERS)
                if attend:
                    nc.tensor.matmul(bank[:, 0:TW], same[:, :], msg[:, :], start=True, stop=True).then_inc(summed, 1)
                else:
                    nc.tensor.matmul(bank[:, 0:YW], same[:, :], rows_in[:, :], start=True, stop=True).then_inc(summed, 1)

            over_chunks(pe, chunk)

        @block.vector
        def _(dve):
            chain = Chain(dve, dve_steps)
            dve.wait_ge(cols_in, 32)
            chain.step(nc.vector.tensor_scalar(low_cols[:, :], dst_cols[:, :], float(NP - 1), None, ALU.min))
            nc.vector.tensor_copy(dst_f[:, :], dst_cols[:, :]).then_inc(low_ready, 1)
            dve.wait_ge(low_ready, 1)
            dve.wait_ge(consts, 1)

            def chunk(k):
                at = bass.ds(k, 1)
                dve.wait_ge(row_in, k * 16 + 16)
                chunk_before(dve, k)
                chain.step(nc.vector.tensor_scalar(same[:, :], dst_row[:, :], dst_f[:, at], None, ALU.is_equal))
                chain.step(nc.vector.tensor_tensor(before[:, :], same[:, :], lower[:, :], ALU.mult))
                chain.step(nc.vector.tensor_reduce(dup[:, :], before[:, :], AX.X, ALU.max))
                chain.step(nc.vector.scalar_tensor_tensor(target[:, :], dup[:, :], float(2 * PAD_DST), dst_f[:, at], ALU.mult, ALU.add))
                if attend:
                    dve.wait_ge(got, k * (16 * GATHERS) + 16 * GATHERS)
                    chain.step(nc.vector.tensor_tensor(prod[:, :], rows_in[:, 0:D], q_rows[:, :], ALU.mult))
                    chain.step(nc.vector.tensor_reduce(score[:, :], prod[:, :].rearrange("p (h d) -> p h d", h=H), AX.X, ALU.add))
                    chain.step(nc.vector.tensor_scalar(score[:, :], score[:, :], float(DH) ** -0.5, None, ALU.mult))
                    nc.vector.tensor_scalar(score[:, :], score[:, :], -5.0, 5.0, ALU.max, ALU.min).then_inc(clip_ready, 1)
                    dve.wait_ge(exp_ready, k + 1)
                    nc.vector.tensor_tensor(msg[:, 0:D].rearrange("p (h d) -> p h d", h=H),
                                            rows_in[:, D:2 * D].rearrange("p (h d) -> p h d", h=H),
                                            msg[:, D:TW].unsqueeze(2).to_broadcast([P, H, DH]), ALU.mult).then_inc(msg_ready, 1)
                    dve.wait_ge(summed, k + 1)
                    nc.vector.tensor_tensor(new[:, :], bank[:, 0:TW], old[:, :], ALU.add).then_inc(new_ready, 1)
                else:
                    nc.vector.tensor_reduce(count[:, :], same[:, :], AX.X, ALU.add).then_inc(msg_ready, 1)
                    dve.wait_ge(msg_ready, k + 1)
                    dve.wait_ge(summed, k + 1)
                    dve.wait_ge(got, k * (16 * GATHERS) + 16 * GATHERS)
                    chain.step(nc.vector.tensor_reduce(part_sum[:, :], bank[:, 0:YW].rearrange("p (k d) -> p d k", k=PARTS), AX.X, ALU.add))
                    chain.step(nc.vector.tensor_tensor(new[:, 0:D], part_sum[:, :], old[:, 0:D], ALU.add))
                    nc.vector.tensor_scalar(new[:, D:TW], old[:, D:TW], count[:, :], None, ALU.add).then_inc(new_ready, 1)

            chunk(0)
            chain.loop(NCE - 1, chain.steps - 1, lambda k: chunk(k + 1))


def sum_by_edge(nc, t, v, work, bank, table, tag):
    room = Room(work, 4 * (YW + H))
    with ExitStack() as stack:
        add_by_edge(nc, t, v, room.take, stack, tag, bank, table)


def attention_by_edge(nc, t, v, work):
    with ExitStack() as ctx:
        room = Room(work)
        sums = room.take("sums", [P, 2, NP])
        with ExitStack() as edge:
            sb, ps, sem = phase(nc, edge, clear=True)
            qt, q = sb("gq_t", [P, D]), sb("gq", [P, D])
            bank, = ps("gq_bank", 1)
            ld, done, copied, st, held = (sem(f"gq_{n}") for n in ("ld", "done", "copied", "st", "held"))
            with nc.Block() as block:
                @block.sync
                def _(sp):
                    with sp.Fori(0, NT) as k:
                        sp.dma_start(qt[:, :], v.qt[:, bass.ds(k * P, P)]).then_inc(ld, 16)
                        sp.wait_ge(copied, k + 1)
                        sp.sem_inc(held, 1)
                        sp.dma_start(v.q_table[bass.ds(k * P, P), :], q[:, :]).then_inc(st, 16)
                        sp.wait_ge(st, k * 16 + 16)
                        sp.sem_inc(held, 1)

                @block.tensor
                def _(pe):
                    with pe.Fori(0, NT) as k:
                        pe.wait_ge(ld, k * 16 + 16)
                        nc.tensor.transpose(bank[:, 0:P], qt[:, :], v.ident[:, :]).then_inc(done, 1)

                @block.scalar
                def _(act):
                    with act.Fori(0, NT) as k:
                        act.wait_ge(done, k + 1)
                        nc.scalar.activation(q[:, :], bank[:, 0:P], ACT.Copy).then_inc(copied, 1)

        with ExitStack() as edge:
            bank = edge.enter_context(nc.psum_tensor("ga_bank", [P, 512], F32))
            add_by_edge(nc, t, v, room.take, edge, "_a", bank)

        with ExitStack() as edge:
            sb, ps, sem = phase(nc, edge, clear=True)
            rows_, wide = sb("gs_rows", [P, TW]), sb("gs_wide", [P, D])
            bank, = ps("gs_bank", 1)
            ld, widened, done, copied, held = (sem(f"gs_{n}") for n in ("ld", "widened", "done", "copied", "held"))
            with nc.Block() as block:
                @block.sync
                def _(sp):
                    sp.dma_start(rows_[:, :], v.totals[0:P, :]).then_inc(ld, 16)
                    with sp.Fori(1, NT) as k:
                        sp.wait_ge(copied, k)
                        sp.sem_inc(held, 1)
                        sp.dma_start(rows_[:, :], v.totals[bass.ds(k * P, P), :]).then_inc(ld, 16)

                @block.vector
                def _(dve):
                    with dve.Fori(0, NT) as k:
                        dve.wait_ge(ld, k * 16 + 16)
                        nc.vector.tensor_copy(wide[:, :].rearrange("p (h d) -> p h d", h=H),
                                              rows_[:, D:TW].unsqueeze(2).to_broadcast([P, H, DH])).then_inc(widened, 1)

                @block.tensor
                def _(pe):
                    with pe.Fori(0, NT) as k:
                        pe.wait_ge(widened, k + 1)
                        nc.tensor.transpose(bank[:, 0:P], rows_[:, 0:D], v.ident[:, :])
                        nc.tensor.transpose(bank[:, P:2 * P], wide[:, :], v.ident[:, :]).then_inc(done, 1)

                @block.scalar
                def _(act):
                    with act.Fori(0, NT) as k:
                        act.wait_ge(done, k + 1)
                        nc.scalar.activation(sums[:, :, bass.ds(k * P, P)], bank[:, 0:2 * P].rearrange("p (a n) -> p a n", a=2),
                                             ACT.Copy).then_inc(copied, 1)

        finish(nc, t, v, sums, "_by_edge")


def finish(nc, t, v, sums, tag=""):
    with ExitStack() as ctx:
        sb, ps, sem = phase(nc, ctx, tag)

        RING = 4
        FIRST, SECOND, LAST = 1, 2, 4

        def sems(name):
            return [sem(f"{name}{i}") for i in range(RING)]

        wo = sb("wo", [P, D])
        vectors = {n: sb(f"f_{n}", [P, D]) for n in ("bo", "gamma1", "beta1", "gamma2", "beta2")}
        inv_root = sb("f_inv_root", [P, 1])
        h_in, x_in = sb("f_h", [P, RING, D]), sb("f_x", [P, RING, D])
        attn = sb("f_attn", [P, 2, D])
        den, inv = sb("f_den", [P, D]), sb("f_inv", [P, D])
        h1 = sb("f_h1", [P, RING, D])
        h2 = sb("f_h2", [P, RING, D])
        n2 = sb("f_n2", [P, RING, D])
        n2T = sb("f_n2T", [P, 2, D])
        prod, total = sb("f_prod", [P, 2, D]), sb("f_total", [P, 2, D])
        ones_row = sb("f_ones", [1, P])
        res = sb("f_res", [P, RING, D])
        stat = sb("f_stat", [P, 2, RING, 12])
        BN, MV, VE, RSTD = slice(0, 6), slice(6, 8), 8, 9
        a_bank, b_bank, c_bank = ps("fa_bank", 2), ps("fb_bank", 2), ps("fc_bank", 2)
        w_in, consts = sem("f_w_in"), sem("f_consts")
        h_ld, x_ld, st = sems("f_h_ld"), sems("f_x_ld"), sems("f_st")
        attn_ready, a_done, a_read, norm2_ready, n2_ready, b_done, n2T_ready, c_done, prod_ready, total_ready, res_ready = (
            sem(f"f_{n}") for n in ("attn_ready", "a_done", "a_read", "norm2_ready", "n2_ready",
                                    "b_done", "n2T_ready", "c_done", "prod_ready", "total_ready", "res_ready"))
        var_ready, rstd_ready = ([sem(f"f_{n}{i}") for i in range(2)] for n in ("var_ready", "rstd_ready"))
        dve_steps, pool_steps, act_steps, sp_steps = (sem(f"f_{n}") for n in ("dve", "pool", "act", "sp"))
        held = sem("f_held")
        block = ctx.enter_context(nc.Block())

        @block.sync
        def _(sp):
            sp.dma_start(wo[:, :], t["L3_gnn_Wo"]).then_inc(w_in, 16)
            for n, tile in vectors.items():
                sp.dma_start(tile[:, :], t[f"L3_gnn_{n}"].partition_broadcast(P)).then_inc(w_in, 16)

            def load_h(dt):
                (dt - (RING - 1)).count(sp, a_read, held)
                sp.dma_start(h_in[:, dt.slot(RING), :], rows(v.h, dt)).then_inc(h_ld[dt.slot(RING)], 16)

            def load_x(dt):
                (dt - (RING - 1)).count(sp, res_ready, held)
                sp.dma_start(x_in[:, dt.slot(RING), :], rows(v.x[2], dt)).then_inc(x_ld[dt.slot(RING)], 16)

            def store(dt, n=P):
                (dt + 1).count(sp, res_ready, held)
                sp.dma_start(t["out"][bass.ds(dt.value(P), n), :], res[0:n, dt.slot(RING), :]).then_inc(st[dt.slot(RING)], 16)

            def step(dt):
                stage(load_h, dt, 0)
                stage(load_x, dt, 1)
                stage(store, dt, LAST)

            over_tiles(Chain(sp, sp_steps), step, LAST - 1)
            store(Num(NT - 1), N - (NT - 1) * P)
            for back in range(RING):
                Num(NT - 1 - back).landed(sp, st, held)

        @block.gpsimd
        def _(pool):
            chain = Chain(pool, pool_steps)
            chain.step(nc.gpsimd.memset(ones_row[:, :], 1.0))
            nc.gpsimd.memset(inv_root[:, :], -0.5).then_inc(consts, 1)
            pool.wait_ge(consts, 1)
            pool.wait_ge(w_in, 16 * 6)

            def deviation(i):
                def one(dt):
                    s = stat[:, i, dt.slot(RING), :]
                    (dt + 1).count(pool, var_ready[i], held)
                    chain.step(nc.gpsimd.tensor_scalar(s[:, VE:VE + 1], s[:, MV.start + 1:MV.stop], EPS_LN, None, ALU.add))
                    nc.gpsimd.tensor_tensor(s[:, RSTD:RSTD + 1], s[:, VE:VE + 1], inv_root[:, :], ALU.pow).then_inc(rstd_ready[i], 1)

                return one

            def scale(dt):
                n2_now = n2[:, dt.slot(RING), :]
                (dt + 1).count(pool, norm2_ready)
                chain.step(nc.gpsimd.tensor_tensor(n2_now, n2_now, vectors["gamma2"][:, :], ALU.mult))
                nc.gpsimd.tensor_tensor(n2_now, n2_now, vectors["beta2"][:, :], ALU.add).then_inc(n2_ready, 1)

            def result(dt):
                (dt + 1).count(pool, total_ready)
                dt.landed(pool, x_ld)
                (dt - RING).landed(pool, st)
                nc.gpsimd.tensor_tensor(res[:, dt.slot(RING), :], total[:, dt.slot(), :], x_in[:, dt.slot(RING), :],
                                        ALU.add).then_inc(res_ready, 1)

            def step(dt):
                stage(deviation(0), dt, FIRST)
                stage(scale, dt, SECOND + 1)
                stage(result, dt, LAST)
                stage(deviation(1), dt, SECOND)

            over_tiles(chain, step, LAST)

        @block.tensor
        def _(pe):
            pe.wait_ge(w_in, 16 * 6)
            pe.wait_ge(consts, 1)

            def transpose_values(dt):
                (dt + 1).count(pe, attn_ready)
                (dt - 1).count(pe, a_read)
                nc.tensor.transpose(a_bank[dt.slot()][:, 0:P], attn[:, dt.slot(), :], v.ident[:, :]).then_inc(a_done, 1)

            def transpose_normed(dt):
                (dt + 1).count(pe, n2_ready)
                (dt - 1).count(pe, n2T_ready)
                nc.tensor.transpose(b_bank[dt.slot()][:, 0:P], n2[:, dt.slot(RING), :], v.ident[:, :]).then_inc(b_done, 1)

            def product(dt):
                (dt + 1).count(pe, n2T_ready)
                (dt - 1).count(pe, prod_ready)
                nc.tensor.matmul(c_bank[dt.slot()][:, 0:D], n2T[:, dt.slot(), :], wo[:, :], start=True, stop=False)
                nc.tensor.matmul(c_bank[dt.slot()][:, 0:D], ones_row[:, :], vectors["bo"][0:1, :], start=False,
                                 stop=True).then_inc(c_done, 1)

            def step(dt):
                stage(transpose_values, dt, 0)
                stage(transpose_normed, dt, SECOND + 1)
                stage(product, dt, SECOND + 1)

            over_tiles(Chain(pe, sp_steps), step, LAST)

        @block.scalar
        def _(act):
            def copy(dt):
                (dt + 1).count(act, b_done)
                (dt - 1).count(act, c_done)
                nc.scalar.activation(n2T[:, dt.slot(), :], b_bank[dt.slot()][:, 0:P], ACT.Copy).then_inc(n2T_ready, 1)

            def relu(dt):
                (dt + 1).count(act, c_done)
                (dt - 1).count(act, total_ready)
                nc.scalar.activation(prod[:, dt.slot(), :], c_bank[dt.slot()][:, 0:D], ACT.Relu).then_inc(prod_ready, 1)

            def step(dt):
                stage(relu, dt, LAST)
                stage(copy, dt, SECOND + 1)

            over_tiles(Chain(act, act_steps), step, LAST)

        @block.vector
        def _(dve):
            chain = Chain(dve, dve_steps)
            dve.wait_ge(w_in, 16 * 6)

            def step(dt):
                values, first, second, third, last = (dt - lag for lag in range(5))
                on = [exists(dt, lag) for lag in range(5)]
                s0, s1 = stat[:, 0, first.slot(RING), :], stat[:, 1, second.slot(RING), :]
                h1_now, h2_now = h1[:, first.slot(RING), :], h2[:, second.slot(RING), :]

                def normed(x, tile, i, y):
                    s = stat[:, i, tile.slot(RING), :]
                    (tile + 1).count(dve, rstd_ready[i])
                    return nc.vector.tensor_scalar(y, x, s[:, MV.start:MV.start + 1], s[:, RSTD:RSTD + 1], ALU.subtract, ALU.mult)

                if on[2]:
                    n1_step = chain.start(normed(h1[:, second.slot(RING), :], second, 0, h2_now))
                if on[1]:
                    (first + 1).count(dve, a_done)
                    first.landed(dve, h_ld)
                    nc.vector.tensor_tensor(h1_now, a_bank[first.slot()][:, 0:P], h_in[:, first.slot(RING), :],
                                            ALU.add).then_inc(a_read, 1)
                if on[0]:
                    at = bass.ds(values.value(P), P)
                    den_step = chain.start(nc.vector.tensor_scalar(den[:, :], sums[:, 1, at], 0.001, None, ALU.add))
                if on[2]:
                    chain.wait(n1_step)
                    gamma_step = chain.start(nc.vector.tensor_tensor(h2_now, h2_now, vectors["gamma1"][:, :], ALU.mult))
                if on[0]:
                    chain.wait(den_step)
                    inv_step = chain.start(nc.vector.reciprocal(inv[:, :], den[:, :]))
                if on[1]:
                    (first + 1).count(dve, a_read)
                    bn0_step = chain.start(nc.vector.bn_stats(s0[:, BN], h1_now))
                if on[0]:
                    chain.wait(inv_step)
                    (values - 1).count(dve, a_done)
                    nc.vector.tensor_tensor(attn[:, values.slot(), :], sums[:, 0, at], inv[:, :],
                                            ALU.mult).then_inc(attn_ready, 1)
                if on[2]:
                    chain.wait(gamma_step)
                    beta_step = chain.start(nc.vector.tensor_tensor(h2_now, h2_now, vectors["beta1"][:, :], ALU.add))
                if on[1]:
                    chain.wait(bn0_step)
                    dve.sem_inc(held, 1)
                    nc.vector.bn_aggr(s0[:, MV], s0[:, BN]).then_inc(var_ready[0], 1)
                if on[3]:
                    (third - (RING - 1)).count(dve, b_done)
                    normed(h2[:, third.slot(RING), :], third, 1, n2[:, third.slot(RING), :]).then_inc(norm2_ready, 1)
                if on[2]:
                    chain.wait(beta_step)
                    bn1_step = chain.start(nc.vector.bn_stats(s1[:, BN], h2_now))
                if on[4]:
                    (last + 1).count(dve, prod_ready)
                    (last - 1).count(dve, res_ready)
                    nc.vector.tensor_tensor(total[:, last.slot(), :], prod[:, last.slot(), :], h2[:, last.slot(RING), :],
                                            ALU.add).then_inc(total_ready, 1)
                if on[2]:
                    chain.wait(bn1_step)
                    dve.sem_inc(held, 1)
                    nc.vector.bn_aggr(s1[:, MV], s1[:, BN]).then_inc(var_ready[1], 1)

            over_tiles(chain, step, LAST)


TRANSPOSED = ("L0_gnn_Wl1", "L0_gnn_Wr1", "L0_gnn_Wl2", "L0_gnn_Wr2", "L2_gnn_W_neigh1", "L2_gnn_W_self1",
              "L2_gnn_W_neigh2", "L2_gnn_W_self2", "L2_gnn_W_neigh3", "L2_gnn_W_self3")


def kernel(**inputs):
    import numpy as np
    import concourse.bacc as bacc
    from concourse.bass_utils import run_bass_kernel_spmd

    arrays = {}
    for name, a in inputs.items():
        a = np.asarray(a)
        if name == "x":
            a = np.pad(a, ((0, NP - N), (0, 0)))
        elif name == "src":
            a = np.pad(a, (0, NC * P - E)).reshape(NC, P).T
            name = "src_cols"
        elif name == "dst":
            arrays["dst_flat"] = np.pad(a, (0, NC * P + 2 * P - E), constant_values=PAD_DST)
            a = arrays["dst_flat"][0:NC * P]
            arrays["dst_rows"] = np.ascontiguousarray(a.reshape(P, CR * P))
            a = a.reshape(NC, P).T
            name = "dst_cols"
        elif name in TRANSPOSED:
            a = a.T
        arrays[name] = np.ascontiguousarray(a)

    nc = bacc.Bacc("TRN2", target_bir_lowering=False, num_devices=1)
    t = {n: nc.dram_tensor(f"in_{n}", a.shape, mybir.dt.from_np(a.dtype), kind="ExternalInput").ap() for n, a in arrays.items()}
    t["out"] = nc.dram_tensor("out", (N, D), F32, kind="ExternalOutput").ap()
    program(nc, t)
    r = run_bass_kernel_spmd(nc, [{f"in_{n}": a for n, a in arrays.items()}], core_ids=[0])
    return r.results[0]["out"]
```
